# Optimizing a Trainium2 kernel written in Bass

```python
import numpy as np
import jax
import jax.numpy as jnp

def _softmax(x, axis=-1):
    return jax.nn.softmax(x, axis=axis)

def _gelu(x):
    return jax.nn.gelu(x, approximate=True)

def _silu(x):
    return jax.nn.silu(x)

def _sigmoid(x):
    return jax.nn.sigmoid(x)

def _layernorm(x, axis=-1, eps=1e-05):
    m = jnp.mean(x, axis=axis, keepdims=True)
    v = jnp.var(x, axis=axis, keepdims=True)
    return (x - m) / jnp.sqrt(v + eps)

def _scatter_add(tgt, idx, src, axis=0):
    return tgt.at[idx].add(src)

def _segment_sum(src, seg, n):
    return jax.ops.segment_sum(src, seg, n)
kernel_name = 'mk_gnn_preln_d2_gnn_r64_bb7b1e'

def setup_inputs(seed: int=0):
    np.random.seed(seed)
    _w = jnp.asarray

    def _rec_inputs():
        import jax
        import jax.numpy as jnp
        _gk = jax.random.key(seed)
        x = -0.000202 + 1 * jax.random.normal(jax.random.fold_in(_gk, 1), (100000, 128), jnp.float32)
        src = jax.random.randint(jax.random.fold_in(_gk, 2), (50000,), 0, 100000, jnp.int32)
        dst = jnp.minimum((100000 * jax.random.uniform(jax.random.fold_in(_gk, 3), (50000,)) ** 2.0).astype(jnp.int32), 99999)
        _o = jnp.argsort(dst, stable=True)
        src = src[_o]
        dst = dst[_o]
        return (x, src, dst)
    x, src, dst = _rec_inputs()

    def _L0_gnn_setup():
        import jax, jax.numpy as jnp
        import numpy as np
        N_NODES = 50000
        N_EDGES = 25000
        D_FEAT = 128
        EMB = 32
        HEADS = 4
        SLOPE = 0.2

        def _gatv2_layer(x, src, dst, W_l, W_r, att, bias, n_nodes):
            H, C = att.shape
            xl = (x @ W_l).reshape(n_nodes, H, C)
            xr = (x @ W_r).reshape(n_nodes, H, C)
            msg = xl[src] + xr[dst]
            e = jnp.einsum('ehc,hc->eh', jax.nn.leaky_relu(msg, SLOPE), att)
            m = jax.ops.segment_max(e, dst, num_segments=n_nodes)
            ex = jnp.exp(e - m[dst])
            denom = jax.ops.segment_sum(ex, dst, num_segments=n_nodes)
            alpha = ex / (denom[dst] + 1e-16)
            out = jax.ops.segment_sum(alpha[:, :, None] * xl[src], dst, num_segments=n_nodes)
            return out.reshape(n_nodes, H * C) + bias
        key = jax.random.key(seed)
        ks = jax.random.split(key, 12)
        H, C = (HEADS, EMB)
        hid = H * C

        def glorot(k, shape):
            fan_in, fan_out = (shape[0], shape[-1] if len(shape) > 1 else shape[0])
            lim = jnp.sqrt(6.0 / (fan_in + fan_out)).astype(jnp.float32)
            return jax.random.uniform(k, shape, jnp.float32, -lim, lim)
        x = jax.random.normal(ks[0], (N_NODES, D_FEAT), jnp.float32)
        edge_index = jax.random.randint(ks[1], (2, N_EDGES), 0, N_NODES, jnp.int32).astype(jnp.int64)
        return {'x': x, 'edge_index': edge_index, 'W1_l': glorot(ks[2], (D_FEAT, hid)), 'W1_r': glorot(ks[3], (D_FEAT, hid)), 'att1': glorot(ks[4], (H, C)), 'b1': jnp.zeros((hid,), jnp.float32), 'W2_l': glorot(ks[5], (hid, hid)), 'W2_r': glorot(ks[6], (hid, hid)), 'att2': glorot(ks[7], (H, C)), 'b2': jnp.zeros((hid,), jnp.float32)}
    _L0_gnn_all = _L0_gnn_setup()
    _L0_gnn_in = {k: v for k, v in _L0_gnn_all.items() if k in ('W1_l', 'W1_r', 'att1', 'b1', 'W2_l', 'W2_r', 'att2', 'b2')}
    del _L0_gnn_all

    def _L1_gnn_setup():
        import jax, jax.numpy as jnp
        import numpy as np
        N, D, E, SDIM = (100000, 128, 8000, 4)
        R = D // 4
        HID = 4 * D

        def _layernorm(x, g, b, eps=1e-05):
            mu = jnp.mean(x, axis=-1, keepdims=True)
            var = jnp.var(x, axis=-1, keepdims=True)
            return (x - mu) * jax.lax.rsqrt(var + eps) * g + b
        key = jax.random.key(seed)
        ks = jax.random.split(key, 20)
        lin = lambda k, out, inp: jax.random.normal(k, (out, inp), jnp.float32) * (1.0 / np.sqrt(inp))
        return {'x': jax.random.normal(ks[0], (N, D), jnp.float32), 'edge_index': jax.random.randint(ks[1], (2, E), 0, N, jnp.int64), 'ln1_g': jnp.ones((D,), jnp.float32), 'ln1_b': jnp.zeros((D,), jnp.float32), 'ln2_g': jnp.ones((D,), jnp.float32), 'ln2_b': jnp.zeros((D,), jnp.float32), 'WQ': lin(ks[2], D, D), 'WK': lin(ks[3], D, D), 'WV': lin(ks[4], D, D), 'WS': lin(ks[5], D, SDIM), 'WE': lin(ks[6], D, D), 'w_a': jax.random.normal(ks[7], (D,), jnp.float32) / np.sqrt(D), 'w_g': jnp.zeros((D,), jnp.float32), 'b_g': jnp.zeros((D,), jnp.float32), 'ffn_w1': lin(ks[8], HID, D), 'ffn_b1': jnp.zeros((HID,), jnp.float32), 'ffn_w2': lin(ks[9], D, HID), 'ffn_b2': jnp.zeros((D,), jnp.float32), 'se_w1': lin(ks[10], R, D), 'se_b1': jnp.zeros((R,), jnp.float32), 'se_w2': lin(ks[11], D, R), 'se_b2': jnp.zeros((D,), jnp.float32)}
    _L1_gnn_all = _L1_gnn_setup()
    _L1_gnn_in = {k: v for k, v in _L1_gnn_all.items() if k in ('ln1_g', 'ln1_b', 'ln2_g', 'ln2_b', 'WQ', 'WK', 'WV', 'WS', 'WE', 'w_a', 'w_g', 'b_g', 'ffn_w1', 'ffn_b1', 'ffn_w2', 'ffn_b2', 'se_w1', 'se_b1', 'se_w2', 'se_b2')}
    del _L1_gnn_all
    return {'x': x, 'src': src, 'dst': dst, 'L0_gnn_W1_l': _L0_gnn_in['W1_l'], 'L0_gnn_W1_r': _L0_gnn_in['W1_r'], 'L0_gnn_att1': _L0_gnn_in['att1'], 'L0_gnn_b1': _L0_gnn_in['b1'], 'L0_gnn_W2_l': _L0_gnn_in['W2_l'], 'L0_gnn_W2_r': _L0_gnn_in['W2_r'], 'L0_gnn_att2': _L0_gnn_in['att2'], 'L0_gnn_b2': _L0_gnn_in['b2'], 'L1_gnn_ln1_g': _L1_gnn_in['ln1_g'], 'L1_gnn_ln1_b': _L1_gnn_in['ln1_b'], 'L1_gnn_ln2_g': _L1_gnn_in['ln2_g'], 'L1_gnn_ln2_b': _L1_gnn_in['ln2_b'], 'L1_gnn_WQ': _L1_gnn_in['WQ'], 'L1_gnn_WK': _L1_gnn_in['WK'], 'L1_gnn_WV': _L1_gnn_in['WV'], 'L1_gnn_WS': _L1_gnn_in['WS'], 'L1_gnn_WE': _L1_gnn_in['WE'], 'L1_gnn_w_a': _L1_gnn_in['w_a'], 'L1_gnn_w_g': _L1_gnn_in['w_g'], 'L1_gnn_b_g': _L1_gnn_in['b_g'], 'L1_gnn_ffn_w1': _L1_gnn_in['ffn_w1'], 'L1_gnn_ffn_b1': _L1_gnn_in['ffn_b1'], 'L1_gnn_ffn_w2': _L1_gnn_in['ffn_w2'], 'L1_gnn_ffn_b2': _L1_gnn_in['ffn_b2'], 'L1_gnn_se_w1': _L1_gnn_in['se_w1'], 'L1_gnn_se_b1': _L1_gnn_in['se_b1'], 'L1_gnn_se_w2': _L1_gnn_in['se_w2'], 'L1_gnn_se_b2': _L1_gnn_in['se_b2']}

def reference(x, src, dst, L0_gnn_W1_l, L0_gnn_W1_r, L0_gnn_att1, L0_gnn_b1, L0_gnn_W2_l, L0_gnn_W2_r, L0_gnn_att2, L0_gnn_b2, L1_gnn_ln1_g, L1_gnn_ln1_b, L1_gnn_ln2_g, L1_gnn_ln2_b, L1_gnn_WQ, L1_gnn_WK, L1_gnn_WV, L1_gnn_WS, L1_gnn_WE, L1_gnn_w_a, L1_gnn_w_g, L1_gnn_b_g, L1_gnn_ffn_w1, L1_gnn_ffn_b1, L1_gnn_ffn_w2, L1_gnn_ffn_b2, L1_gnn_se_w1, L1_gnn_se_b1, L1_gnn_se_w2, L1_gnn_se_b2):
    import jax
    import jax.numpy as jnp

    def _L0_gnn_ref(x, edge_index, W1_l, W1_r, att1, b1, W2_l, W2_r, att2, b2):
        import jax, jax.numpy as jnp
        import numpy as np
        N_NODES = 50000
        N_EDGES = 25000
        D_FEAT = 128
        EMB = 32
        HEADS = 4
        SLOPE = 0.2

        def _gatv2_layer(x, src, dst, W_l, W_r, att, bias, n_nodes):
            H, C = att.shape
            xl = (x @ W_l).reshape(n_nodes, H, C)
            xr = (x @ W_r).reshape(n_nodes, H, C)
            msg = xl[src] + xr[dst]
            e = jnp.einsum('ehc,hc->eh', jax.nn.leaky_relu(msg, SLOPE), att)
            m = jax.ops.segment_max(e, dst, num_segments=n_nodes)
            ex = jnp.exp(e - m[dst])
            denom = jax.ops.segment_sum(ex, dst, num_segments=n_nodes)
            alpha = ex / (denom[dst] + 1e-16)
            out = jax.ops.segment_sum(alpha[:, :, None] * xl[src], dst, num_segments=n_nodes)
            return out.reshape(n_nodes, H * C) + bias
        n = x.shape[0]
        loop = jnp.arange(n, dtype=edge_index.dtype)
        src = jnp.concatenate([edge_index[0], loop])
        dst = jnp.concatenate([edge_index[1], loop])
        h = jax.nn.relu(_gatv2_layer(x, src, dst, W1_l, W1_r, att1, b1, n))
        h = jax.nn.relu(_gatv2_layer(h, src, dst, W2_l, W2_r, att2, b2, n))
        return h

    def _L1_gnn_ref(x, edge_index, ln1_g, ln1_b, ln2_g, ln2_b, WQ, WK, WV, WS, WE, w_a, w_g, b_g, ffn_w1, ffn_b1, ffn_w2, ffn_b2, se_w1, se_b1, se_w2, se_b2):
        import jax, jax.numpy as jnp
        import numpy as np
        N, D, E, SDIM = (100000, 128, 8000, 4)
        R = D // 4
        HID = 4 * D

        def _layernorm(x, g, b, eps=1e-05):
            mu = jnp.mean(x, axis=-1, keepdims=True)
            var = jnp.var(x, axis=-1, keepdims=True)
            return (x - mu) * jax.lax.rsqrt(var + eps) * g + b
        n = x.shape[0]
        src, dst = (edge_index[0], edge_index[1])
        h = _layernorm(x, ln1_g, ln1_b)
        Q, K, V = (h @ WQ.T, h @ WK.T, h @ WV.T)
        deg = x[:, -4]
        coords = x[:, -3:]
        s_concat = jnp.concatenate([(deg[dst] - deg[src])[:, None], coords[dst] - coords[src]], axis=-1)
        xi = jax.nn.relu(Q[dst] + K[src] + s_concat @ WS.T)
        logits = xi @ w_a
        max_per = jnp.full((n,), -1e+30, x.dtype).at[dst].max(logits)
        exp_s = jnp.exp(logits - max_per[dst])
        denom = jnp.zeros((n,), x.dtype).at[dst].add(exp_s)
        alpha = exp_s / (denom[dst] + 1e-09)
        v_mix = V[src] + xi @ WE.T
        z = jnp.zeros_like(x).at[dst].add(alpha[:, None] * v_mix)
        gate = jax.nn.sigmoid(deg[:, None] * w_g + b_g)
        z = z * (1.0 + gate)
        y = x + z
        h2 = _layernorm(y, ln2_g, ln2_b)
        ffn = jax.nn.gelu(h2 @ ffn_w1.T + ffn_b1, approximate=False) @ ffn_w2.T + ffn_b2
        y2 = y + ffn
        g = jnp.mean(y2, axis=0, keepdims=True)
        s = jax.nn.sigmoid(jax.nn.relu(g @ se_w1.T + se_b1) @ se_w2.T + se_b2)
        return y2 * s
    edge_index = jnp.stack([src, dst])
    h = jnp.maximum(_layernorm(x, axis=-1), 0.0)
    x = x + _L0_gnn_ref(h, edge_index, L0_gnn_W1_l, L0_gnn_W1_r, L0_gnn_att1, L0_gnn_b1, L0_gnn_W2_l, L0_gnn_W2_r, L0_gnn_att2, L0_gnn_b2)
    h = jnp.maximum(_layernorm(x, axis=-1), 0.0)
    x = x + _L1_gnn_ref(h, edge_index, L1_gnn_ln1_g, L1_gnn_ln1_b, L1_gnn_ln2_g, L1_gnn_ln2_b, L1_gnn_WQ, L1_gnn_WK, L1_gnn_WV, L1_gnn_WS, L1_gnn_WE, L1_gnn_w_a, L1_gnn_w_g, L1_gnn_b_g, L1_gnn_ffn_w1, L1_gnn_ffn_b1, L1_gnn_ffn_w2, L1_gnn_ffn_b2, L1_gnn_se_w1, L1_gnn_se_b1, L1_gnn_se_w2, L1_gnn_se_b2)
    return x

_drawn_inputs = setup_inputs


def setup_inputs(seed=0):
    import zlib

    import numpy as np

    out = dict(_drawn_inputs(seed))
    spreads = {'L0_gnn_b1': (0.0, 0.1),
     'L0_gnn_b2': (0.0, 0.1),
     'L1_gnn_ln1_g': (1.0, 0.2),
     'L1_gnn_ln1_b': (0.0, 0.1),
     'L1_gnn_ln2_g': (1.0, 0.2),
     'L1_gnn_ln2_b': (0.0, 0.318),
     'L1_gnn_w_g': (0.0, 0.8),
     'L1_gnn_b_g': (0.0, 0.8),
     'L1_gnn_ffn_b1': (0.0, 0.334),
     'L1_gnn_ffn_b2': (0.0, 0.1),
     'L1_gnn_se_b1': (0.0, 0.501),
     'L1_gnn_se_b2': (0.0, 0.29)}
    factors = {'L0_gnn_W1_r': 6.071, 'L0_gnn_W2_r': 8.0, 'L0_gnn_att2': 5.193}
    for name, (base, spread) in spreads.items():
        noise = np.random.default_rng([zlib.crc32(name.encode()), seed]).standard_normal(out[name].shape)
        drawn = base * np.exp(spread * noise) if base else spread * noise
        out[name] = jnp.asarray(drawn.astype(out[name].dtype))
    for name, factor in factors.items():
        out[name] = (out[name] * factor).astype(out[name].dtype)
    return out
```

```python
from contextlib import ExitStack

import concourse.bass as bass
from concourse import mybir
from concourse.alu_op_type import AluOpType as ALU

F32 = mybir.dt.float32
I32 = mybir.dt.int32
ACT = mybir.ActivationFunctionType
AX = mybir.AxisListType

P = 128
J = 4
GROUP = P * J
EP = 125
B = 4
SLOTS = 4
NEG = -1.0e30
SKIP = 4.0e6
EPS = 1.0e-5


class Step:

    def __init__(self, m, k, wk, off, unroll, last):
        self.m, self.k, self.wk, self.last = m, k, wk, last
        self.slot, self.wslot = off % SLOTS, off % unroll
        self.first = isinstance(m, int) and m == 0


def run_steps(eng, count, stages, unroll=SLOTS):
    deepest = max(lag for lag, _ in stages)
    head = -(-deepest // unroll) * unroll + unroll
    turns = max(0, (count - 1 - head) // unroll)

    def straight(n):
        for lag, fn in stages:
            m = n - lag
            if 0 <= m < count:
                fn(Step(m, m // SLOTS, m // unroll, m, unroll, m == count - 1))

    if turns == 0:
        for n in range(count + deepest):
            straight(n)
        return
    for n in range(head):
        straight(n)
    with eng.Fori(0, turns) as i:
        for u in range(unroll):
            for lag, fn in stages:
                off = head + u - lag
                fn(Step(i * unroll + off, i * (unroll // SLOTS) + off // SLOTS, i + off // unroll, off, unroll, False))
    for n in range(head + turns * unroll, count + deepest):
        straight(n)


def stand_alone(eng, passed):
    eng.sem_inc(passed, 1)


def need(eng, sem, value):
    if not (isinstance(value, int) and value <= 0):
        eng.wait_ge(sem, value)


def moments(v, c, bn, mean, vpe, tmp):
    m0, q0, m1, q1 = bn[:, :, 1], bn[:, :, 2], bn[:, :, 4], bn[:, :, 5]
    c.put(v.tensor_tensor(tmp[:, 0], m0, m1, ALU.add))
    c.put(v.tensor_tensor(tmp[:, 1], m0, m1, ALU.subtract))
    c.put(v.tensor_tensor(tmp[:, 2], q0, q1, ALU.add))
    c.sync()
    c.put(v.tensor_scalar(mean, tmp[:, 0], 0.5, None, ALU.mult))
    c.put(v.tensor_tensor(tmp[:, 1], tmp[:, 1], tmp[:, 1], ALU.mult))
    c.sync()
    c.put(v.scalar_tensor_tensor(tmp[:, 2], tmp[:, 1], P / 4.0, tmp[:, 2], ALU.mult, ALU.add))
    c.sync()
    c.put(v.tensor_scalar(vpe, tmp[:, 2], 1.0 / P, EPS, ALU.mult, ALU.add))


def clear_semaphores(nc, sems):
    nums = sorted(x.num for x in sems)
    starts = [n for n in nums if n - 1 not in nums]
    with nc.Block() as block:
        @block.sync
        def _(sp):
            for n in starts:
                end = n
                while end in nums:
                    end += 1
                sp.sem_clear(range(n, end))


class Chain:

    def __init__(self, eng, sem):
        self.eng, self.sem, self.base, self.n = eng, sem, 0, 0

    def at(self, base):
        self.base, self.n = base, 0
        return self

    def put(self, ins):
        self.n += 1
        return ins.then_inc(self.sem, 1)

    def sync(self):
        self.eng.wait_ge(self.sem, self.base + self.n)


def join_pieces(nc, k, tag, H, C, state, F, ctx, sem, after_steps, finish):
    HW = H * (C + 1)
    dgm, m1, m2 = (ctx.enter_context(nc.sbuf_tensor(tag + n, [EP, H, EP], F32)) for n in ("j_diag", "j_m1", "j_m2"))
    G, Q, QE = (ctx.enter_context(nc.sbuf_tensor(tag + n, [EP, 3 * H], F32)) for n in ("j_max", "j_arg", "j_exp"))
    TS, f1, f2 = (ctx.enter_context(nc.sbuf_tensor(tag + n, [EP, HW], F32)) for n in ("j_scaled", "j_f1", "j_f2"))
    FX = ctx.enter_context(nc.sbuf_tensor(tag + "j_total", [EP, 2, HW], F32))
    j_vec, j_diag, j_max, j_arg, j_exp, j_scaled, j_sum, j_rows = (
        sem(n) for n in ("j_vec", "j_diag_ready", "j_max_ready", "j_arg_ready", "j_exp_ready", "j_scaled_ready", "j_sum_ready", "j_rows_ready"))
    T_ = state

    def heads(ap):
        return ap.rearrange("p (h c) -> p h c", h=H)

    def over(ap, n):
        return ap.unsqueeze(2).to_broadcast([EP, H, n])

    def vec(v, out):
        c = Chain(v, j_vec)
        v.wait_ge(*after_steps)
        for h in range(H):
            c.put(v.tensor_scalar(dgm[:, h], k.ident[0:EP, 0:EP], T_[:, HW + h:HW + h + 1], None, ALU.mult))
        c.sync()
        v.sem_inc(j_diag, 1)
        v.wait_ge(j_max, 1)
        rows = k.join_ps[0][0:EP, 0:H * EP].rearrange("p (h q) -> p h q", h=H)
        c.put(v.tensor_tensor(m1[:, :, :], rows, k.NT[:, :].unsqueeze(1).to_broadcast([EP, H, EP]), ALU.add))
        c.put(v.tensor_tensor(m2[:, :, :], rows, k.NBm[:, :].unsqueeze(1).to_broadcast([EP, H, EP]), ALU.add))
        c.sync()
        c.put(v.tensor_reduce(G[:, 0:H], m1[:, :, :], AX.X, ALU.max))
        c.put(v.tensor_reduce(G[:, H:2 * H], m2[:, :, :], AX.X, ALU.max))
        c.sync()
        c.put(v.tensor_tensor(G[:, 2 * H:3 * H], F[:, HW:HW + H], G[:, H:2 * H], ALU.max))
        c.put(v.tensor_tensor(Q[:, 0:H], T_[:, HW:HW + H], G[:, 0:H], ALU.subtract))
        c.sync()
        c.put(v.tensor_tensor(Q[:, H:2 * H], F[:, HW:HW + H], G[:, 2 * H:3 * H], ALU.subtract))
        c.put(v.tensor_tensor(Q[:, 2 * H:3 * H], G[:, H:2 * H], G[:, 2 * H:3 * H], ALU.subtract))
        c.sync()
        v.sem_inc(j_arg, 1)
        v.wait_ge(j_exp, 1)
        c.put(v.tensor_tensor(heads(TS[:, :]), heads(T_[:, 0:HW]), over(QE[:, 0:H], C + 1), ALU.mult))
        c.put(v.tensor_tensor(heads(f1[:, :]), heads(F[:, 0:HW]), over(QE[:, H:2 * H], C + 1), ALU.mult))
        c.sync()
        v.sem_inc(j_scaled, 1)
        v.wait_ge(j_sum, 1)
        c.put(v.tensor_copy(FX[:, 0], k.join_ps[1][0:EP, 0:HW]))
        c.put(v.tensor_tensor(heads(f2[:, :]), heads(k.join_ps[1][0:EP, 256:256 + HW]), over(QE[:, 2 * H:3 * H], C + 1), ALU.mult))
        c.sync()
        c.put(v.tensor_tensor(FX[:, 1], f1[:, :], f2[:, :], ALU.add))
        c.sync()
        finish(v, c, FX[:, :, :].rearrange("p n (h c) -> p n h c", h=H), 2, out)
        c.sync()
        v.sem_inc(j_rows, 1)

    def pe(_):
        nc.tensor.wait_ge(j_diag, 1)
        for h in range(H):
            last = nc.tensor.matmul(k.join_ps[0][0:EP, h * EP:(h + 1) * EP], k.ones[0:EP, 0:EP], dgm[:, h], start=True, stop=True)
        last.then_inc(j_max, 1)
        nc.tensor.wait_ge(j_scaled, 1)
        nc.tensor.matmul(k.join_ps[1][0:EP, 0:HW], k.ET[:, :], TS[:, :], start=True, stop=True)
        nc.tensor.matmul(k.join_ps[1][0:EP, 256:256 + HW], k.EA[:, :], TS[:, :], start=True, stop=True).then_inc(j_sum, 1)

    def act(act_):
        act_.wait_ge(j_arg, 1)
        act_.activation(QE[:, :], Q[:, :], ACT.Exp).then_inc(j_exp, 1)

    def pool(pool_, out, table, done, last_row):
        pool_.wait_ge(j_rows, 1)
        for n in range(2):
            pool_.indirect_dma_start(table, bass.IndirectOffsetOnAxis(k.idxP[:, n:n + 1], 0), out[:, n], None,
                                     bounds_check=last_row, oob_is_err=False).then_inc(done, 16)
        pool_.wait_ge(done, 32)

    return vec, pe, act, pool


def gather(pool, to, table, index, last_row):
    return pool.indirect_dma_start(to, None, table, bass.IndirectOffsetOnAxis(index, 0), bounds_check=last_row, oob_is_err=False)


def gat_layer(nc, k, layer, src_t, dst_t, out_t, res_t, Wl, Wr, attc, brow):
    H, C = 4, 32
    HW = H * (C + 1)
    HS = HW + H
    T, NB, N = k.T, k.NB, k.N
    K_ARGS = 7 + B
    K_MAIN = 5 + 3 * B + 5
    used = []
    with ExitStack() as ctx, ExitStack() as blocks:
        def sb(name, shape, dt=F32):
            return ctx.enter_context(nc.sbuf_tensor(f"g{layer}_{name}", list(shape), dt))

        def sem(name):
            used.append(ctx.enter_context(nc.semaphore(f"{name}_{layer}")))
            return used[-1]

        IB = sb("IB", [EP, SLOTS, B, 2], I32)
        OB = sb("OB", [EP, SLOTS, B], I32)
        FB = sb("FB", [EP, SLOTS, B, 3])
        DW = 2 * P if layer == 1 else P
        XS, XD = sb("XS", [EP, SLOTS, B, P]), sb("XD", [EP, SLOTS, B, DW])
        XR = sb("XR", [EP, SLOTS, B, P]) if res_t is not None else None
        sdT = sb("sdT", [P, 2, 2, B * EP])
        lr = sb("lr", [P, 2, 2, 2, B * EP])
        EM = sb("EM", [EP, SLOTS, B, H])
        D1 = sb("D1", [EP, SLOTS, B, H])
        MH = sb("MH", [EP, SLOTS, B + 1, H])
        CB = sb("CB", [EP, SLOTS, B, H])
        A = sb("A", [EP, SLOTS, B, 3 * H])
        XE = sb("XE", [EP, SLOTS, B, 3 * H])
        Wt = sb("Wt", [EP, 2, B, HW])
        W2 = sb("W2", [EP, 2, B, P])
        prod = sb("prod", [EP, HW])
        ST = sb("ST", [EP, SLOTS, B, HS])
        F = sb("F", [EP, HS])
        den = sb("den", [EP, 2, B, H])
        O = sb("O", [EP, SLOTS, B, P])
        OJ, XJ = sb("OJ", [EP, 2, P]), sb("XJ", [EP, 2, P])
        zero = sb("zero", [P, k.ZR]) if layer == 1 else None
        pS, pD = (ctx.enter_context(nc.psum_tensor(f"g{layer}_{n}", [P, 512], F32)) for n in ("pS", "pD"))
        pV, pU, pL = ([ctx.enter_context(nc.psum_tensor(f"g{layer}_{n}{i}", [P, 512], F32)) for i in range(2)] for n in ("pV", "pU", "pL"))
        gat = [sem(f"gat{s}") for s in range(SLOTS)]
        rows_out = [sem(f"rows_out{s}") for s in range(SLOTS)]
        idx_in, flags_in, tr_done, sdT_ready, mm_done, v_done, lr_ready, lg_done, exp_done, args_steps, main_steps, init, join_in, join_out, clr, zero_made, passed = (
            sem(n) for n in ("idx_in", "flags_in", "tr_done", "sdT_ready", "mm_done", "v_done", "lr_ready", "lg_done", "exp_done",
                             "args_steps", "main_steps", "init", "join_in", "join_out", "z_cleared", "zero_made", "passed"))
        gathers = 2 * B
        xe_rows = k.xe_t.rearrange("(p t) f -> p t f", t=T)
        xe = [sem(f"xe{s}") for s in range(SLOTS)]
        k.join_ps = (pS, pD)

        def heads(ap):
            return ap.rearrange("p t (h c) -> p t h c", h=H)

        def over(ap, n):
            return ap.unsqueeze(3).to_broadcast([EP, B, H, n])

        def finish(v, c, acc, n, out, dn, xr):
            c.put(v.tensor_scalar(dn, acc[:, :, :, C], 1e-16, None, ALU.add))
            c.sync()
            c.put(v.reciprocal(dn, dn))
            c.sync()
            c.put(v.tensor_tensor(out.rearrange("p t (h c) -> p t h c", h=H), acc[:, :, :, 0:C],
                                  dn.unsqueeze(3).to_broadcast([EP, n, H, C]), ALU.mult))
            c.sync()
            c.put(v.tensor_tensor(out, out, brow[0:EP, :].unsqueeze(1).to_broadcast([EP, n, P]), ALU.add))
            c.sync()
            if xr is None:
                c.put(v.tensor_scalar(out, out, 0.0, None, ALU.max))
            else:
                c.put(v.scalar_tensor_tensor(out, out, 0.0, xr, ALU.max, ALU.add))

        join_vec, join_pe, join_act, join_pool = join_pieces(
            nc, k, f"g{layer}_", H, C, ST[:, (NB - 1) % SLOTS, B - 1], F, ctx, sem, (main_steps, NB * K_MAIN),
            lambda v, c, acc, n, out: finish(v, c, acc, n, out, den[:, 0, 0:2], XJ[:, :, :] if res_t is not None else None))
        block = blocks.enter_context(nc.Block())

        @block.sync
        def _(sp):
            if zero is not None:
                sp.wait_ge(zero_made, 1)
                n = k.z_rows // k.ZR
                with sp.Fori(0, n) as i:
                    sp.dma_start(k.z_t[bass.ds(i * k.ZR, k.ZR), :].rearrange("(p j) f -> p (j f)", p=P), zero[:, :]).then_inc(clr, 16)

            def keep_x(st):
                sp.wait_ge(gat[st.slot], 16 * gathers * (st.k + 1))
                sp.dma_start(xe_rows[:, bass.ds(st.m * B, B), :], XD[:, st.slot, :, P:2 * P]).then_inc(xe[st.slot], 16)

            def load_x(st):
                need(sp, main_steps, (st.m - 3) * K_MAIN)
                sp.dma_start(XR[:, st.slot], xe_rows[:, bass.ds(st.m * B, B), :]).then_inc(xe[st.slot], 16)

            run_steps(sp, NB, [(0, keep_x if layer == 1 else load_x)])
            if zero is not None:
                sp.wait_ge(clr, 16 * (k.z_rows // k.ZR))
            for s in range(SLOTS):
                sp.wait_ge(xe[s], 16 * ((NB - 1 - s) // SLOTS + 1))

        @block.gpsimd
        def _(pool):
            if zero is not None:
                pool.memset(zero[:, :], 0.0).then_inc(zero_made, 1)

            last_row = pool.to_reg(N - 1)
            last_source = pool.to_reg(2 * N - 1) if layer == 1 else last_row

            def fetch(st):
                s = st.slot
                need(pool, gat[s], 16 * gathers * st.k)
                pool.tensor_copy(IB[:, s], k.idx[:, bass.ds(st.m * B, B), (2 if layer == 1 else 0):(4 if layer == 1 else 2)]).then_inc(idx_in, 1)
                pool.wait_ge(idx_in, st.m + 1)
                need(pool, tr_done, st.m - 3)
                if layer == 1:
                    need(pool, xe[s], 16 * st.k)
                stand_alone(pool, passed)
                for t in range(B):
                    gather(pool, XS[:, s, t], src_t, IB[:, s, t, 0:1], last_source).then_inc(gat[s], 16)
                    gather(pool, XD[:, s, t], dst_t, IB[:, s, t, 1:2], last_row).then_inc(gat[s], 16)

            def flags(st):
                s = st.slot
                need(pool, rows_out[s], 16 * B * st.k)
                pool.tensor_copy(OB[:, s], k.idx[:, bass.ds(st.m * B, B), 4])
                need(pool, main_steps, (st.m - 3) * K_MAIN)
                pool.tensor_copy(FB[:, s], k.flag[:, bass.ds(st.m * B, B), :]).then_inc(flags_in, 1)

            def write_rows(st):
                pool.wait_ge(flags_in, st.m + 1)
                pool.wait_ge(main_steps, (st.m + 1) * K_MAIN)
                stand_alone(pool, passed)
                for t in range(B):
                    pool.indirect_dma_start(out_t, bass.IndirectOffsetOnAxis(OB[:, st.slot, t:t + 1], 0), O[:, st.slot, t], None,
                                            bounds_check=last_row, oob_is_err=False).then_inc(rows_out[st.slot], 16)

            run_steps(pool, NB, [(0, fetch), (1, flags), (3, write_rows)])
            if res_t is not None:
                gather(pool, XJ[:, 0], res_t, k.idx[:, T - 1, 1:2], last_row).then_inc(join_in, 16)
                gather(pool, XJ[:, 1], res_t, k.idx[:, 0, 1:2], last_row).then_inc(join_in, 16)
            join_pool(pool, OJ, out_t, join_out, last_row)
            for s in range(SLOTS):
                pool.wait_ge(rows_out[s], 16 * B * ((NB - 1 - s) // SLOTS + 1))

        @block.tensor
        def _(pe):
            def turn(st):
                s = st.slot
                pe.wait_ge(gat[s], 16 * gathers * (st.k + 1))
                need(pe, lr_ready, st.m)
                for to, rows in ((pS, XS), (pD, XD[:, :, :, 0:P])):
                    for t in range(B):
                        last = nc.tensor.transpose(to[:, t * EP:(t + 1) * EP], rows[:, s, t], k.ident[0:EP, 0:EP])
                last.then_inc(tr_done, 1)

            def project(st):
                p = st.slot % 2
                pe.wait_ge(sdT_ready, st.m + 1)
                sT, dT = sdT[:, p, 0], sdT[:, p, 1]
                nc.tensor.matmul(pS[:, 0:B * EP], Wl[:, :], sT, start=True, stop=False)
                nc.tensor.matmul(pS[:, 0:B * EP], Wr[:, :], dT, start=False, stop=True)
                nc.tensor.matmul(pD[:, 0:B * EP], Wl[:, :], dT, start=True, stop=False)
                nc.tensor.matmul(pD[:, 0:B * EP], Wr[:, :], dT, start=False, stop=True).then_inc(mm_done, 1)
                need(pe, main_steps, (st.m - 2) * K_MAIN + 4)
                for t in range(B):
                    nc.tensor.matmul(pV[p][0:EP, t * P:(t + 1) * P], sT[:, t * EP:(t + 1) * EP], Wl[:, :], start=True, stop=True)
                    last = nc.tensor.matmul(pU[p][0:EP, t * P:(t + 1) * P], dT[:, t * EP:(t + 1) * EP], Wl[:, :], start=True, stop=True)
                last.then_inc(v_done, 1)

            def logits(st):
                p = st.slot % 2
                pe.wait_ge(lr_ready, st.m + 1)
                need(pe, args_steps, (st.m - 1) * K_ARGS)
                for t in range(B):
                    for i in range(2):
                        to = pL[p][0:EP, (2 * t + i) * H:(2 * t + i + 1) * H]
                        nc.tensor.matmul(to, lr[:, p, i, 0, t * EP:(t + 1) * EP], attc[:, 0:H], start=True, stop=False)
                        last = nc.tensor.matmul(to, lr[:, p, i, 1, t * EP:(t + 1) * EP], attc[:, H:2 * H], start=False, stop=True)
                last.then_inc(lg_done, 1)

            run_steps(pe, NB, [(0, turn), (1, logits), (0, project)])
            join_pe(pe)

        @block.scalar
        def _(act):
            def relu_rows(st):
                p = st.slot % 2
                act.wait_ge(tr_done, st.m + 1)
                need(act, v_done, st.m - 1)
                act.activation(sdT[:, p, 0], pS[:, 0:B * EP], ACT.Relu)
                act.activation(sdT[:, p, 1], pD[:, 0:B * EP], ACT.Relu).then_inc(sdT_ready, 1)

            def leaky(st):
                p = st.slot % 2
                act.wait_ge(mm_done, st.m + 1)
                need(act, lg_done, st.m - 1)
                for i, of in enumerate((pS, pD)):
                    act.activation(lr[:, p, i, 0], of[:, 0:B * EP], ACT.Relu)
                    last = act.activation(lr[:, p, i, 1], of[:, 0:B * EP], ACT.Relu, scale=-1.0)
                last.then_inc(lr_ready, 1)

            def exps(st):
                act.wait_ge(args_steps, (st.m + 1) * K_ARGS)
                need(act, main_steps, (st.m - 3) * K_MAIN)
                act.activation(XE[:, st.slot], A[:, st.slot], ACT.Exp).then_inc(exp_done, 1)

            run_steps(act, NB, [(0, relu_rows), (1, exps), (0, leaky)])
            join_act(act)

        @block.vector
        def _(v):
            v.memset(MH[:, SLOTS - 1], 0.0).then_inc(init, 1)
            v.memset(ST[:, SLOTS - 1], 0.0).then_inc(init, 1)
            v.memset(F[:, :], 0.0).then_inc(init, 1)
            v.wait_ge(init, 3)
            ca, cm = Chain(v, args_steps), Chain(v, main_steps)

            def args(st):
                s, prev, p = st.slot, (st.slot - 1) % SLOTS, st.slot % 2
                v.wait_ge(lg_done, st.m + 1)
                v.wait_ge(flags_in, st.m + 1)
                need(v, args_steps, st.m * K_ARGS)
                need(v, exp_done, st.m - 3)
                c = ca.at(st.m * K_ARGS)
                lg = pL[p][0:EP, 0:2 * H * B].rearrange("p (t i h) -> p t i h", t=B, i=2)
                c.put(v.tensor_copy(MH[:, s, 0], MH[:, prev, B]))
                c.put(v.tensor_tensor(EM[:, s], lg[:, :, 1], FB[:, s, :, 1].unsqueeze(2).to_broadcast([EP, B, H]), ALU.add))
                c.sync()
                c.put(v.tensor_tensor(D1[:, s], lg[:, :, 0], EM[:, s], ALU.max))
                c.sync()
                for t in range(B):
                    c.put(v.scalar_tensor_tensor(MH[:, s, t + 1], MH[:, s, t], FB[:, s, t, 0:1], D1[:, s, t], ALU.add, ALU.max))
                    c.sync()
                c.put(v.tensor_tensor(CB[:, s], MH[:, s, 0:B], FB[:, s, :, 0].unsqueeze(2).to_broadcast([EP, B, H]), ALU.add))
                c.put(v.tensor_tensor(A[:, s, :, 0:H], lg[:, :, 0], MH[:, s, 1:B + 1], ALU.subtract))
                c.put(v.tensor_tensor(A[:, s, :, H:2 * H], EM[:, s], MH[:, s, 1:B + 1], ALU.subtract))
                c.sync()
                c.put(v.tensor_tensor(A[:, s, :, 2 * H:3 * H], CB[:, s], MH[:, s, 1:B + 1], ALU.subtract))
                assert c.n == K_ARGS, c.n

            def main(st):
                s, prev, p = st.slot, (st.slot - 1) % SLOTS, st.slot % 2
                v.wait_ge(exp_done, st.m + 1)
                v.wait_ge(v_done, st.m + 1)
                if res_t is not None:
                    v.wait_ge(xe[st.slot], 16 * (st.k + 1))
                need(v, main_steps, st.m * K_MAIN)
                c = cm.at(st.m * K_MAIN)
                w = heads(Wt[:, p])
                ex, sf = XE[:, s, :, 0:H], XE[:, s, :, H:2 * H]
                c.put(v.tensor_tensor(w[:, :, :, 0:C], heads(pV[p][0:EP, :].rearrange("p (t f) -> p t f", t=B)), over(ex, C), ALU.mult))
                c.put(v.tensor_tensor(heads(W2[:, p]), heads(pU[p][0:EP, :].rearrange("p (t f) -> p t f", t=B)), over(sf, C), ALU.mult))
                c.put(v.tensor_tensor(w[:, :, :, C], ex, sf, ALU.add))
                c.put(v.tensor_copy(ST[:, s, :, HW:HS], MH[:, s, 1:B + 1]))
                c.sync()
                c.put(v.tensor_tensor(w[:, :, :, 0:C], w[:, :, :, 0:C], heads(W2[:, p]), ALU.add))
                for t in range(B):
                    before = ST[:, s, t - 1, 0:HW] if t else ST[:, prev, B - 1, 0:HW]
                    c.put(v.tensor_tensor(prod[:, :].rearrange("p (h c) -> p h c", h=H), before.rearrange("p (h c) -> p h c", h=H),
                                          XE[:, s, t, 2 * H:3 * H].unsqueeze(2).to_broadcast([EP, H, C + 1]), ALU.mult))
                    c.sync()
                    c.put(v.tensor_tensor(ST[:, s, t, 0:HW], prod[:, :], Wt[:, p, t], ALU.add))
                    c.sync()
                    c.put(v.scalar_tensor_tensor(F[:, :], ST[:, s, t], FB[:, s, t, 2:3], F[:, :], ALU.mult, ALU.add))
                need(v, rows_out[s], 16 * B * st.k)
                finish(v, c, heads(ST[:, s, :, 0:HW]), B, O[:, s], den[:, p], None if res_t is None else XR[:, s])
                assert c.n == K_MAIN, c.n

            run_steps(v, NB, [(2, main), (1, args)])
            if res_t is not None:
                v.wait_ge(join_in, 32)
            join_vec(v, OJ[:, :, :])

        blocks.close()
        clear_semaphores(nc, used)


def edge_attention(nc, k):
    H, C = 1, P
    HW, HS = C + 1, C + 2
    T, NB, N = k.T, k.NB, k.N
    R = 2 * B
    K_TAKE = R + 8
    K_CENTRE = R + 10
    K_SCALE = 5
    K_ARGS = 3 + B + 1
    K_MAIN = 3 + 2 * B + 4
    W = k.W
    used = []
    with ExitStack() as ctx, ExitStack() as blocks:
        def sb(name, shape, dt=F32):
            return ctx.enter_context(nc.sbuf_tensor("e_" + name, list(shape), dt))

        def sem(name):
            used.append(ctx.enter_context(nc.semaphore(name + "_e")))
            return used[-1]

        IB = sb("IB", [EP, SLOTS, B, 2], I32)
        OB = sb("OB", [EP, SLOTS, B], I32)
        FB = sb("FB", [EP, SLOTS, B, 3])
        XX = sb("XX", [EP, SLOTS, R, P])
        bn = sb("bn", [EP, 2, R, 6])
        tmpm = sb("tmpm", [EP, 3, R])
        mean, vpe, mu, vu, r1, r2, rr = (sb(n, [EP, SLOTS, R]) for n in ("mean", "vpe", "mu", "vu", "r1", "r2", "rr"))
        nmean, nmr = sb("nmean", [EP, SLOTS, R]), sb("nmr", [EP, SLOTS, R])
        g4 = sb("g4", [EP, SLOTS, R, 4])
        ex6 = sb("ex6", [EP, SLOTS, B, 6])
        dg = sb("deg_ends", [EP, 2])
        GE = sb("GE", [EP, SLOTS, B, P])
        hT = sb("hT", [P, 2, 2, B * EP])
        exT = sb("exT", [6, 2, B * EP])
        xiT = sb("xiT", [P, 2, B * EP])
        MH = sb("MH", [EP, SLOTS, B + 1])
        CB = sb("CB", [EP, SLOTS, B])
        A, XE = sb("A", [EP, SLOTS, 2, B]), sb("XE", [EP, SLOTS, 2, B])
        Wt = sb("Wt", [EP, 2, B, HW])
        ST = sb("ST", [EP, SLOTS, B, HS])
        F = sb("F", [EP, HS])
        den = sb("den", [EP, 2, B])
        O = sb("O", [EP, SLOTS, B, P])
        OJ, GJ = sb("OJ", [EP, 2, P]), sb("GJ", [EP, 2, P])
        pS, pD, pX, pG = (ctx.enter_context(nc.psum_tensor("e_" + n, [P, 512], F32)) for n in ("pS", "pD", "pX", "pG"))
        pV, pL = ([ctx.enter_context(nc.psum_tensor(f"e_{n}{i}", [P, 512], F32)) for i in range(2)] for n in ("pV", "pL"))
        gat = [sem(f"gat{s}") for s in range(SLOTS)]
        rows_out = [sem(f"rows_out{s}") for s in range(SLOTS)]
        (idx_in, flags_in, r1_in, r2_in, tr_done, hT_ready, mm_done, xi_ready, v_done, exp_done,
         take_steps, centre_steps, scale_steps, args_steps, main_steps, init, join_out, gj_arg, gj_exp, passed, u_ready, h_ready, gate_done) = (
            sem(n) for n in ("idx_in", "flags_in", "r1_in", "r2_in", "tr_done", "hT_ready", "mm_done", "xi_ready", "v_done",
                             "exp_done", "take_steps", "centre_steps", "scale_steps", "args_steps", "main_steps", "init", "join_out",
                             "gj_arg", "gj_exp", "passed", "u_ready", "h_ready", "gate_done"))
        k.join_ps = (pS, pD)

        def finish(v, c, acc, n, out, dn, ge):
            c.put(v.tensor_scalar(dn, acc[:, :, C], 1e-9, 2.0, ALU.add, ALU.mult))
            c.sync()
            c.put(v.reciprocal(dn, dn))
            c.sync()
            c.put(v.tensor_tensor(out, acc[:, :, 0:C], dn.unsqueeze(2).to_broadcast([EP, n, C]), ALU.mult))
            c.sync()
            c.put(v.scalar_tensor_tensor(out, ge, 3.0, out, ALU.add, ALU.mult))

        def join_finish(v, c, acc, n, out):
            for i in range(2):
                c.put(v.scalar_tensor_tensor(GJ[:, i], k.row["w_g"][0:EP, :], dg[:, i:i + 1], k.row["b_g"][0:EP, :], ALU.mult, ALU.add))
            c.sync()
            v.sem_inc(gj_arg, 1)
            v.wait_ge(gj_exp, 1)
            finish(v, c, acc.rearrange("p n h c -> p n (h c)"), n, out, den[:, 0, 0:2], GJ[:, :, :])

        join_vec, join_pe, join_act, join_pool = join_pieces(
            nc, k, "e_", H, C, ST[:, (NB - 1) % SLOTS, B - 1], F, ctx, sem, (main_steps, NB * K_MAIN), join_finish)
        block = blocks.enter_context(nc.Block())

        @block.gpsimd
        def _(pool):
            last_row = pool.to_reg(N - 1)

            def fetch(st):
                s = st.slot
                need(pool, gat[s], 16 * R * st.k)
                pool.tensor_copy(IB[:, s], k.idx[:, bass.ds(st.m * B, B), 0:2]).then_inc(idx_in, 1)
                pool.wait_ge(idx_in, st.m + 1)
                need(pool, tr_done, st.m - 3)
                stand_alone(pool, passed)
                for t in range(B):
                    for i in range(2):
                        gather(pool, XX[:, s, i * B + t], k.x1_t, IB[:, s, t, i:i + 1], last_row).then_inc(gat[s], 16)

            def rsqrt1(st):
                pool.wait_ge(take_steps, (st.m + 1) * K_TAKE)
                pool.tensor_tensor(r1[:, st.slot], vpe[:, st.slot], k.half[0:EP, 0:R], ALU.pow).then_inc(r1_in, 1)

            def rsqrt2(st):
                pool.wait_ge(centre_steps, (st.m + 1) * K_CENTRE)
                pool.tensor_tensor(r2[:, st.slot], vu[:, st.slot], k.half[0:EP, 0:R], ALU.pow).then_inc(r2_in, 1)

            def flags(st):
                s = st.slot
                need(pool, rows_out[s], 16 * B * st.k)
                pool.tensor_copy(OB[:, s], k.idx[:, bass.ds(st.m * B, B), 4])
                need(pool, main_steps, (st.m - 3) * K_MAIN)
                pool.tensor_copy(FB[:, s], k.flag[:, bass.ds(st.m * B, B), :]).then_inc(flags_in, 1)

            def write_rows(st):
                pool.wait_ge(flags_in, st.m + 1)
                pool.wait_ge(main_steps, (st.m + 1) * K_MAIN)
                stand_alone(pool, passed)
                for t in range(B):
                    pool.indirect_dma_start(k.z_t[0:N, :], bass.IndirectOffsetOnAxis(OB[:, st.slot, t:t + 1], 0), O[:, st.slot, t], None,
                                            bounds_check=last_row, oob_is_err=False).then_inc(rows_out[st.slot], 16)

            run_steps(pool, NB, [(4, flags), (0, fetch), (2, rsqrt2), (1, rsqrt1), (6, write_rows)])
            join_pool(pool, OJ, k.z_t[0:N, :], join_out, last_row)
            for s in range(SLOTS):
                pool.wait_ge(rows_out[s], 16 * B * ((NB - 1 - s) // SLOTS + 1))

        @block.tensor
        def _(pe):
            def turn(st):
                s = st.slot
                pe.wait_ge(h_ready, st.m + 1)
                need(pe, xi_ready, st.m)
                for i, to in enumerate((pS, pD)):
                    for t in range(B):
                        nc.tensor.transpose(to[:, t * EP:(t + 1) * EP], XX[:, s, i * B + t], k.ident[0:EP, 0:EP])
                for t in range(B):
                    last = nc.tensor.transpose(pX[0:6, t * EP:(t + 1) * EP], ex6[:, s, t], k.ident[0:EP, 0:EP])
                last.then_inc(tr_done, 1)

            def project(st):
                p = st.slot % 2
                pe.wait_ge(hT_ready, st.m + 1)
                nc.tensor.matmul(pS[:, 0:B * EP], W["WQT"][:, :], hT[:, p, 1], start=True, stop=False)
                nc.tensor.matmul(pS[:, 0:B * EP], W["WKT"][:, :], hT[:, p, 0], start=False, stop=False)
                nc.tensor.matmul(pS[:, 0:B * EP], k.WS6[:, :], exT[:, p], start=False, stop=True).then_inc(mm_done, 1)
                need(pe, exp_done, st.m)
                for t in range(B):
                    last = nc.tensor.matmul(pG[0:EP, t * P:(t + 1) * P], exT[:, p, t * EP:(t + 1) * EP], k.WG6[:, :], start=True, stop=True)
                last.then_inc(gate_done, 1)

            def values(st):
                p = st.slot % 2
                pe.wait_ge(xi_ready, st.m + 1)
                need(pe, main_steps, (st.m - 2) * K_MAIN + 3)
                need(pe, args_steps, (st.m - 1) * K_ARGS)
                for t in range(B):
                    xi = xiT[:, p, t * EP:(t + 1) * EP]
                    nc.tensor.matmul(pV[p][0:EP, t * P:(t + 1) * P], hT[:, p, 0, t * EP:(t + 1) * EP], W["WVT"][:, :], start=True, stop=False)
                    nc.tensor.matmul(pV[p][0:EP, t * P:(t + 1) * P], xi, W["WET"][:, :], start=False, stop=True)
                    last = nc.tensor.matmul(pL[p][0:EP, t:t + 1], xi, k.col["w_a"][:, :], start=True, stop=True)
                last.then_inc(v_done, 1)

            run_steps(pe, NB, [(4, values), (3, turn), (3, project)])
            join_pe(pe)

        @block.scalar
        def _(act):
            def affine_rows(st):
                p = st.slot % 2
                act.wait_ge(tr_done, st.m + 1)
                need(act, v_done, st.m - 1)
                for i, of in enumerate((pS, pD)):
                    act.activation(hT[:, p, i], of[:, 0:B * EP], ACT.Identity, bias=k.col["ln1_b"][:, :], scale=k.col["ln1_g"][:, :])
                act.activation(exT[:, p], pX[0:6, 0:B * EP], ACT.Copy).then_inc(hT_ready, 1)

            def relu_xi(st):
                act.wait_ge(mm_done, st.m + 1)
                act.activation(xiT[:, st.slot % 2], pS[:, 0:B * EP], ACT.Relu).then_inc(xi_ready, 1)

            def exps(st):
                s = st.slot
                act.wait_ge(args_steps, (st.m + 1) * K_ARGS)
                need(act, main_steps, (st.m - 3) * K_MAIN)
                act.activation(XE[:, s], A[:, s], ACT.Exp)
                act.wait_ge(gate_done, st.m + 1)
                act.activation(GE[:, s], pG[0:EP, :].rearrange("p (t f) -> p t f", t=B), ACT.Tanh, scale=0.5).then_inc(exp_done, 1)

            def centre_rows(st):
                act.wait_ge(take_steps, (st.m + 1) * K_TAKE)
                for i in range(R):
                    last = act.activation(XX[:, st.slot, i], XX[:, st.slot, i], ACT.Relu, bias=nmean[:, st.slot, i:i + 1])
                last.then_inc(u_ready, 1)

            def scale_rows(st):
                act.wait_ge(scale_steps, (st.m + 1) * K_SCALE)
                for i in range(R):
                    last = act.activation(XX[:, st.slot, i], XX[:, st.slot, i], ACT.Identity, bias=nmr[:, st.slot, i:i + 1],
                                          scale=rr[:, st.slot, i:i + 1])
                last.then_inc(h_ready, 1)

            run_steps(act, NB, [(3, scale_rows), (4, exps), (3, affine_rows), (1, centre_rows), (3, relu_xi)])
            join_act(act)
            act.wait_ge(gj_arg, 1)
            act.activation(GJ[:, :, :], GJ[:, :, :], ACT.Tanh, scale=0.5).then_inc(gj_exp, 1)

        @block.vector
        def _(v):
            v.memset(MH[:, SLOTS - 1], 0.0).then_inc(init, 1)
            v.memset(ST[:, SLOTS - 1], 0.0).then_inc(init, 1)
            v.memset(F[:, :], 0.0).then_inc(init, 1)
            v.memset(ex6[:, :, :, :], 1.0).then_inc(init, 1)
            v.wait_ge(init, 4)
            ct, cc, cs, ca, cm = (Chain(v, x) for x in (take_steps, centre_steps, scale_steps, args_steps, main_steps))

            def take(st):
                s, p = st.slot, st.slot % 2
                v.wait_ge(gat[s], 16 * R * (st.k + 1))
                c = ct.at(st.m * K_TAKE)
                need(v, centre_steps, (st.m - 1) * K_CENTRE)
                for i in range(R):
                    c.put(v.bn_stats(bn[:, p, i], XX[:, s, i]))
                c.sync()
                moments(v, c, bn[:, p], mean[:, s], vpe[:, s], tmpm)
                c.put(v.tensor_scalar(nmean[:, s], tmpm[:, 0], -0.5, None, ALU.mult))
                assert c.n == K_TAKE

            def centre(st):
                s, p = st.slot, st.slot % 2
                v.wait_ge(u_ready, st.m + 1)
                need(v, take_steps, (st.m + 1) * K_TAKE)
                c = cc.at(st.m * K_CENTRE)
                for i in range(R):
                    c.put(v.bn_stats(bn[:, p, i], XX[:, s, i]))
                c.sync()
                moments(v, c, bn[:, p], mu[:, s], vu[:, s], tmpm)
                v.wait_ge(r1_in, st.m + 1)
                c.sync()
                c.put(v.scalar_tensor_tensor(vu[:, s], vu[:, s], -EPS, r1[:, s], ALU.add, ALU.mult))
                c.sync()
                c.put(v.tensor_tensor(vu[:, s], vu[:, s], r1[:, s], ALU.mult))
                c.sync()
                c.put(v.tensor_scalar(vu[:, s], vu[:, s], EPS, None, ALU.add))
                assert c.n == K_CENTRE

            def scale(st):
                s = st.slot
                v.wait_ge(r2_in, st.m + 1)
                need(v, tr_done, st.m - 3)
                c = cs.at(st.m * K_SCALE)
                c.put(v.tensor_tensor(rr[:, s], r2[:, s], r1[:, s], ALU.mult))
                c.put(v.tensor_tensor(g4[:, s], XX[:, s, :, P - 4:P], r1[:, s].unsqueeze(2).to_broadcast([EP, R, 4]), ALU.mult))
                c.sync()
                c.put(v.scalar_tensor_tensor(nmr[:, s], mu[:, s], -1.0, rr[:, s], ALU.mult, ALU.mult))
                c.put(v.tensor_tensor(ex6[:, s, :, 2:6], g4[:, s, B:R], g4[:, s, 0:B], ALU.subtract))
                c.put(v.tensor_copy(ex6[:, s, :, 0], g4[:, s, B:R, 0]))
                if st.first:
                    v.tensor_copy(dg[:, 1:2], g4[:, s, B, 0:1])
                if st.last:
                    v.tensor_copy(dg[:, 0:1], g4[:, s, R - 1, 0:1])
                assert c.n == K_SCALE, c.n

            def args(st):
                s, prev, p = st.slot, (st.slot - 1) % SLOTS, st.slot % 2
                v.wait_ge(v_done, st.m + 1)
                v.wait_ge(flags_in, st.m + 1)
                need(v, args_steps, st.m * K_ARGS)
                need(v, exp_done, st.m - 3)
                c = ca.at(st.m * K_ARGS)
                lg = pL[p][0:EP, 0:B]
                c.put(v.tensor_copy(MH[:, s, 0:1], MH[:, prev, B:B + 1]))
                c.sync()
                for t in range(B):
                    c.put(v.scalar_tensor_tensor(MH[:, s, t + 1:t + 2], MH[:, s, t:t + 1], FB[:, s, t, 0:1], pL[p][0:EP, t:t + 1], ALU.add, ALU.max))
                    c.sync()
                c.put(v.tensor_tensor(CB[:, s], MH[:, s, 0:B], FB[:, s, :, 0], ALU.add))
                c.put(v.tensor_tensor(A[:, s, 0], lg, MH[:, s, 1:B + 1], ALU.subtract))
                c.sync()
                c.put(v.tensor_tensor(A[:, s, 1], CB[:, s], MH[:, s, 1:B + 1], ALU.subtract))
                assert c.n == K_ARGS, c.n

            def main(st):
                s, prev, p = st.slot, (st.slot - 1) % SLOTS, st.slot % 2
                v.wait_ge(exp_done, st.m + 1)
                need(v, main_steps, st.m * K_MAIN)
                c = cm.at(st.m * K_MAIN)
                c.put(v.tensor_tensor(Wt[:, p, :, 0:C], pV[p][0:EP, :].rearrange("p (t f) -> p t f", t=B),
                                      XE[:, s, 0].unsqueeze(2).to_broadcast([EP, B, C]), ALU.mult))
                c.put(v.tensor_copy(Wt[:, p, :, C], XE[:, s, 0]))
                c.put(v.tensor_copy(ST[:, s, :, HW], MH[:, s, 1:B + 1]))
                c.sync()
                for t in range(B):
                    before = ST[:, s, t - 1, 0:HW] if t else ST[:, prev, B - 1, 0:HW]
                    c.put(v.scalar_tensor_tensor(ST[:, s, t, 0:HW], before, XE[:, s, 1, t:t + 1], Wt[:, p, t], ALU.mult, ALU.add))
                    c.sync()
                    c.put(v.scalar_tensor_tensor(F[:, :], ST[:, s, t], FB[:, s, t, 2:3], F[:, :], ALU.mult, ALU.add))
                need(v, rows_out[s], 16 * B * st.k)
                finish(v, c, ST[:, s, :, 0:HW], B, O[:, s], den[:, p], GE[:, s])
                assert c.n == K_MAIN, c.n

            run_steps(v, NB, [(5, main), (4, args), (3, scale), (2, centre), (1, take)])
            join_vec(v, OJ[:, :, :])

        blocks.close()
        clear_semaphores(nc, used)


def ffn_pass(nc, k):
    N, NG = k.N, k.NG
    K_TAKE = J + 7
    K_CENTRE = 3 * J + 7
    K_SCALE = J
    used = []
    with ExitStack() as ctx, ExitStack() as blocks:
        def sb(name, shape, dt=F32):
            return ctx.enter_context(nc.sbuf_tensor("f_" + name, list(shape), dt))

        def sem(name):
            used.append(ctx.enter_context(nc.semaphore(name + "_f")))
            return used[-1]

        X = sb("X", [P, SLOTS, J, P])
        Z, Y, O = (sb(n, [P, SLOTS, J, P]) for n in ("Z", "Y", "O"))
        bn = sb("bn", [P, 2, J, 6])
        tmpm = sb("tmpm", [P, 3, J])
        mean, vpe, mu, vu, r1, r2 = (sb(n, [P, SLOTS, J]) for n in ("mean", "vpe", "mu", "vu", "r1", "r2"))
        HN = sb("HN", [P, 2, J, P])
        hT, fT = sb("hT", [P, 2, GROUP]), sb("fT", [P, 2, GROUP])
        GT = sb("GT", [P, 2, 4, GROUP])
        pT, pF, pN, pG = (ctx.enter_context(nc.psum_tensor("f_" + n, [P, 512], F32)) for n in ("pT", "pF", "pN", "pG"))
        pH = [ctx.enter_context(nc.psum_tensor(f"f_pH{i}", [P, 512], F32)) for i in range(4)]
        rows_in = [sem(f"rows_in{s}") for s in range(SLOTS)]
        y2_out = [sem(f"y2_out{s}") for s in range(SLOTS)]
        (r1_in, r2_in, take_steps, centre_steps, scale_steps, y2_ready, tr_done, hT_ready, up_done, gelu_ready, down_done,
         fT_ready, back_done, sum_done, gsum_in) = (
            sem(n) for n in ("r1_in", "r2_in", "take_steps", "centre_steps", "scale_steps", "y2_ready", "tr_done", "hT_ready",
                             "up_done", "gelu_ready", "down_done", "fT_ready", "back_done", "sum_done", "gsum_in"))
        block = blocks.enter_context(nc.Block())

        @block.sync
        def _(sp):
            def load(st):
                need(sp, centre_steps, (st.m - 3) * K_CENTRE)
                sp.dma_start(X[:, st.slot], k.rows_of(k.x1_t, st)).then_inc(rows_in[st.slot], 16)
                sp.dma_start(Z[:, st.slot], k.rows_of(k.z_t[0:N, :], st)).then_inc(rows_in[st.slot], 16)

            def store(st):
                sp.wait_ge(y2_ready, st.m + 1)
                if st.last:
                    sp.wait_ge(y2_out[(st.m - 1) % SLOTS], 16 * ((st.m - 1) // SLOTS + 1))
                sp.dma_start(k.rows_of(k.y2_t, st), O[:, st.slot]).then_inc(y2_out[st.slot], 16)

            run_steps(sp, NG, [(0, load), (5, store)])
            for s in range(SLOTS):
                sp.wait_ge(y2_out[s], 16 * ((NG - 1 - s) // SLOTS + 1))

        @block.gpsimd
        def _(pool):
            def rsqrt1(st):
                pool.wait_ge(take_steps, (st.m + 1) * K_TAKE)
                pool.tensor_tensor(r1[:, st.slot], vpe[:, st.slot], k.half[:, 0:J], ALU.pow).then_inc(r1_in, 1)

            def rsqrt2(st):
                pool.wait_ge(centre_steps, (st.m + 1) * K_CENTRE)
                pool.tensor_tensor(r2[:, st.slot], vu[:, st.slot], k.half[:, 0:J], ALU.pow).then_inc(r2_in, 1)

            run_steps(pool, NG, [(1, rsqrt2), (0, rsqrt1)])

        @block.vector
        def _(v):
            ct, cc, cs = (Chain(v, x) for x in (take_steps, centre_steps, scale_steps))

            def take(st):
                s, p = st.slot, st.slot % 2
                v.wait_ge(rows_in[s], 32 * (st.k + 1))
                need(v, centre_steps, (st.m - 1) * K_CENTRE)
                c = ct.at(st.m * K_TAKE)
                for j in range(J):
                    c.put(v.bn_stats(bn[:, p, j], X[:, s, j]))
                c.sync()
                moments(v, c, bn[:, p], mean[:, s], vpe[:, s], tmpm)

            def centre(st):
                s, p = st.slot, st.slot % 2
                v.wait_ge(r1_in, st.m + 1)
                c = cc.at(st.m * K_CENTRE)
                for j in range(J):
                    c.put(v.tensor_scalar(X[:, s, j], X[:, s, j], mean[:, s, j:j + 1], 0.0, ALU.subtract, ALU.max))
                c.sync()
                need(v, y2_ready, st.m - 3)
                for j in range(J):
                    c.put(v.scalar_tensor_tensor(Y[:, s, j], X[:, s, j], r1[:, s, j:j + 1], Z[:, s, j], ALU.mult, ALU.add))
                c.sync()
                for j in range(J):
                    c.put(v.bn_stats(bn[:, p, j], Y[:, s, j]))
                c.sync()
                moments(v, c, bn[:, p], mu[:, s], vu[:, s], tmpm)

            def scale(st):
                s, p = st.slot, st.slot % 2
                v.wait_ge(r2_in, st.m + 1)
                need(v, tr_done, st.m - 1)
                c = cs.at(st.m * K_SCALE)
                for j in range(J):
                    c.put(v.tensor_scalar(HN[:, p, j], Y[:, s, j], mu[:, s, j:j + 1], r2[:, s, j:j + 1], ALU.subtract, ALU.mult))

            def add_ffn(st):
                v.wait_ge(back_done, st.m + 1)
                need(v, y2_out[st.slot], 16 * st.k)
                need(v, sum_done, st.m - 3)
                v.tensor_tensor(O[:, st.slot], Y[:, st.slot], pN[:, :].rearrange("p (j f) -> p j f", j=J), ALU.add).then_inc(y2_ready, 1)

            run_steps(v, NG, [(2, scale), (4, add_ffn), (1, centre), (0, take)])
            v.wait_ge(sum_done, NG)
            v.tensor_scalar(k.gsum[:, :], pG[:, 0:1], 1.0 / N, None, ALU.mult).then_inc(gsum_in, 1)
            v.wait_ge(gsum_in, 1)

        @block.tensor
        def _(pe):
            def turn(st):
                p = st.slot % 2
                pe.wait_ge(scale_steps, (st.m + 1) * K_SCALE)
                need(pe, hT_ready, st.m)
                for j in range(J):
                    last = nc.tensor.transpose(pT[:, j * P:(j + 1) * P], HN[:, p, j], k.ident[:, :])
                last.then_inc(tr_done, 1)

            def up(st):
                pe.wait_ge(hT_ready, st.m + 1)
                for c in range(4):
                    need(pe, gelu_ready, (st.m - 1) * 4 + c + 1)
                    nc.tensor.matmul(pH[c][:, :], k.F1T[:, c], hT[:, st.slot % 2], start=True, stop=True).then_inc(up_done, 1)

            def down(st):
                need(pe, fT_ready, st.m)
                for c in range(4):
                    pe.wait_ge(gelu_ready, st.m * 4 + c + 1)
                    last = nc.tensor.matmul(pF[:, :], k.F2T[:, c], GT[:, st.slot % 2, c], start=c == 0, stop=c == 3)
                last.then_inc(down_done, 1)

            def turn_back(st):
                pe.wait_ge(fT_ready, st.m + 1)
                need(pe, y2_ready, st.m)
                for j in range(J):
                    last = nc.tensor.transpose(pN[:, j * P:(j + 1) * P], fT[:, st.slot % 2, j * P:(j + 1) * P], k.ident[:, :])
                last.then_inc(back_done, 1)

            def add_rows(st):
                pe.wait_ge(y2_ready, st.m + 1)
                weights = k.tail_ones[:, 0:1] if st.last else k.ones[:, 0:1]
                for j in range(J):
                    last = nc.tensor.matmul(pG[:, 0:1], O[:, st.slot, j], weights, start=st.first and j == 0, stop=st.last and j == J - 1)
                last.then_inc(sum_done, 1)

            run_steps(pe, NG, [(2, turn), (3, down), (2, up), (3, turn_back), (5, add_rows)])

        @block.scalar
        def _(act):
            def affine(st):
                act.wait_ge(tr_done, st.m + 1)
                need(act, up_done, (st.m - 1) * 4)
                act.activation(hT[:, st.slot % 2], pT[:, :], ACT.Identity, bias=k.col["ln2_b"][:, :], scale=k.col["ln2_g"][:, :]).then_inc(hT_ready, 1)

            def gelu(st):
                need(act, down_done, st.m - 1)
                for c in range(4):
                    act.wait_ge(up_done, st.m * 4 + c + 1)
                    act.activation(GT[:, st.slot % 2, c], pH[c][:, :], ACT.Gelu, bias=k.fb1[:, c:c + 1]).then_inc(gelu_ready, 1)

            def down_bias(st):
                act.wait_ge(down_done, st.m + 1)
                need(act, back_done, st.m - 1)
                act.activation(fT[:, st.slot % 2], pF[:, :], ACT.Identity, bias=k.col["ffn_b2"][:, :]).then_inc(fT_ready, 1)

            run_steps(act, NG, [(2, affine), (3, down_bias), (2, gelu)])

        blocks.close()
        clear_semaphores(nc, used)


def squeeze_and_out(nc, k):
    NG = k.NG
    used = []
    with ExitStack() as ctx, ExitStack() as blocks:
        def sb(name, shape, dt=F32):
            return ctx.enter_context(nc.sbuf_tensor("o_" + name, list(shape), dt))

        def sem(name):
            used.append(ctx.enter_context(nc.semaphore(name + "_o")))
            return used[-1]

        X, Y, O = (sb(n, [P, SLOTS, J, P]) for n in ("X", "Y", "O"))
        s1, s2, s3, nb2 = sb("s1", [32, 1]), sb("s2", [P, 1]), sb("s3", [P, 1]), sb("nb2", [P, 1])
        dg = sb("dg", [P, P])
        ps = ctx.enter_context(nc.psum_tensor("o_ps", [P, 512], F32))
        pr = ctx.enter_context(nc.psum_tensor("o_pr", [P, 512], F32))
        rows_in = [sem(f"rows_in{s}") for s in range(SLOTS)]
        rows_out = [sem(f"rows_out{s}") for s in range(SLOTS)]
        squeeze_pe, squeeze_act, squeeze_vec, mults, sums = (sem(n) for n in ("squeeze_pe", "squeeze_act", "squeeze_vec", "mults", "sums"))
        block = blocks.enter_context(nc.Block())

        @block.sync
        def _(sp):
            def load(st):
                need(sp, sums, st.m - 3)
                sp.dma_start(X[:, st.slot], k.rows_of(k.x1_t, st)).then_inc(rows_in[st.slot], 16)
                sp.dma_start(Y[:, st.slot], k.rows_of(k.y2_t, st)).then_inc(rows_in[st.slot], 16)

            run_steps(sp, NG, [(0, load)])

        @block.tensor
        def _(pe):
            nc.tensor.matmul(ps[0:32, 0:1], k.S1T[:, :], k.gsum[:, :], start=True, stop=True).then_inc(squeeze_pe, 1)
            pe.wait_ge(squeeze_act, 1)
            nc.tensor.matmul(ps[:, 1:2], k.S2T[:, :], s1[:, :], start=True, stop=True).then_inc(squeeze_pe, 1)
            pe.wait_ge(squeeze_vec, 4)
            nc.tensor.matmul(pr[:, 0:P], k.ones[:, :], dg[:, :], start=True, stop=True).then_inc(squeeze_pe, 1)

        @block.scalar
        def _(act):
            act.wait_ge(squeeze_pe, 1)
            act.activation(s1[:, :], ps[0:32, 0:1], ACT.Relu, bias=k.seb1[:, :]).then_inc(squeeze_act, 1)
            act.wait_ge(squeeze_pe, 2)
            act.wait_ge(squeeze_vec, 1)
            act.activation(s2[:, :], ps[:, 1:2], ACT.Exp, scale=-1.0, bias=nb2[:, :]).then_inc(squeeze_act, 1)

            def store(st):
                act.wait_ge(sums, st.m + 1)
                if st.last:
                    act.wait_ge(rows_out[(st.m - 1) % SLOTS], 16 * ((st.m - 1) // SLOTS + 1))
                act.dma_start(k.rows_of(k.a["out"], st), O[:, st.slot]).then_inc(rows_out[st.slot], 16)

            run_steps(act, NG, [(0, store)])
            for s in range(SLOTS):
                act.wait_ge(rows_out[s], 16 * ((NG - 1 - s) // SLOTS + 1))

        @block.vector
        def _(v):
            c = Chain(v, squeeze_vec)
            c.put(v.tensor_scalar(nb2[:, :], k.col["se_b2"][:, :], -1.0, None, ALU.mult))
            v.wait_ge(squeeze_act, 2)
            c.put(v.tensor_scalar(s3[:, :], s2[:, :], 1.0, None, ALU.add))
            c.sync()
            c.put(v.reciprocal(s3[:, :], s3[:, :]))
            c.sync()
            c.put(v.tensor_scalar(dg[:, :], k.ident[:, :], s3[:, :], None, ALU.mult))
            v.wait_ge(squeeze_pe, 3)
            c.put(v.tensor_copy(k.srow[:, :], pr[:, 0:P]))
            c.sync()

            def gated(st):
                s = st.slot
                v.wait_ge(rows_in[s], 32 * (st.k + 1))
                need(v, rows_out[s], 16 * st.k)
                v.tensor_tensor(O[:, s], Y[:, s], k.srow[:, :].unsqueeze(1).to_broadcast([P, J, P]), ALU.mult).then_inc(mults, 1)
                v.wait_ge(mults, st.m + 1)
                v.tensor_tensor(O[:, s], O[:, s], X[:, s], ALU.add).then_inc(sums, 1)

            run_steps(v, NG, [(0, gated)])

        blocks.close()
        clear_semaphores(nc, used)


class Shared:
    pass


def build(nc, N, E, a):
    T = E // EP
    assert T * EP == E and T % B == 0
    NG = -(-N // GROUP)
    TAIL = N - (NG - 1) * GROUP
    NB = T // B
    assert TAIL % J == 0 and N >= GROUP

    def table(name, rows=N):
        return nc.dram_tensor(name, (rows, P), F32).ap()

    h1_t, x1_t, y2_t = (table(n) for n in ("tab_h1", "tab_x1", "tab_y2"))
    xx_t = nc.dram_tensor("tab_xx", (N, 2 * P), F32).ap()
    xe_t = nc.dram_tensor("tab_xe", (E, P), F32).ap()
    ZR = 16 * P
    z_rows = -(-NG * GROUP // ZR) * ZR
    z_t = table("tab_z", z_rows)

    def rows_of(t, st):
        base = N - GROUP if st.last else st.m * GROUP
        return t[bass.ds(base, GROUP), :].rearrange("(p j) f -> p j f", j=J)

    whole = ExitStack()
    with whole:
        def sb(name, shape, dt=F32, ctx=whole):
            return ctx.enter_context(nc.sbuf_tensor(name, list(shape), dt))

        def pb(name, ctx):
            return ctx.enter_context(nc.psum_tensor(name, [P, 512], F32))

        used = []

        def sem(name, ctx):
            used.append(ctx.enter_context(nc.semaphore(name)))
            return used[-1]

        ident = sb("ident", [P, P])
        ones = sb("ones", [P, P])
        tail_ones = sb("tail_ones", [P, 1])
        half = sb("half", [P, 2 * B])
        headmask = sb("headmask", [P, 4])
        W = {n: sb(n, [P, P]) for n in ("W1l", "W1r", "W2l", "W2r", "WQT", "WKT", "WVT", "WET")}
        WS6 = sb("WS6", [6, P])
        WG6 = sb("WG6", [6, P])
        att = [sb("att1c", [P, 8]), sb("att2c", [P, 8])]
        col = {n: sb("c_" + n, [P, 1]) for n in ("b1", "b2", "ln1_g", "ln1_b", "ln2_g", "ln2_b", "w_a", "ffn_b2", "se_b2", "a1", "a2")}
        fb1 = sb("fb1", [P, 4])
        seb1 = sb("seb1", [32, 1])
        F1T = sb("F1T", [P, 4, P])
        F2T = sb("F2T", [P, 4, P])
        S1T = sb("S1T", [P, 32])
        S2T = sb("S2T", [32, P])
        row = {n: sb("r_" + n, [P, P]) for n in ("b1", "b2", "w_g", "b_g")}
        idx = sb("idx", [EP, T, 5], I32)
        flag = sb("flag", [EP, T, 3])
        idxP = sb("idxP", [EP, 2], I32)
        ET = sb("ET", [EP, EP])
        EA = sb("EA", [EP, EP])
        EB = sb("EB", [EP, EP])
        NT = sb("NT", [EP, EP])
        NBm = sb("NBm", [EP, EP])
        srow = sb("srow", [P, P])
        gsum = sb("gsum", [P, 1])

        with ExitStack() as ctx, ExitStack() as blocks:
            raw = {n: sb("raw_" + n, [P, P], ctx=ctx) for n in ("WQ", "WK", "WV", "WE")}
            rawS = sb("rawS", [P, 6], ctx=ctx)
            raw1 = sb("raw1", [P, 4, P], ctx=ctx)
            raw2 = sb("raw2", [P, 512], ctx=ctx)
            rawe1 = sb("rawe1", [32, P], ctx=ctx)
            rawe2 = sb("rawe2", [P, 32], ctx=ctx)
            dint = sb("dint", [EP, T + 2], I32, ctx)
            sint = sb("sint", [EP, T], I32, ctx)
            d = sb("d", [EP, T + 2], ctx=ctx)
            stt, ent, hrt, het, wrt, tmp = (sb(n, [EP, T], ctx=ctx) for n in ("stt", "ent", "hrt", "het", "wrt", "tmp"))
            sm = sb("sm", [EP, 8], ctx=ctx)
            dg = sb("dg", [EP, 2, EP], ctx=ctx)
            drow = sb("drow", [EP, 2, EP], ctx=ctx)
            ps = [pb(f"ps{i}", ctx) for i in range(6)]
            loaded = sem("setup_loaded", ctx)
            edges_in = sem("edges_in", ctx)
            pads = sem("pads", ctx)
            made = sem("consts_made", ctx)
            madeg = sem("consts_steps", ctx)
            turned = sem("weights_turned", ctx)
            vec = sem("setup_vec", ctx)
            diag = sem("diag_ready", ctx)
            drows = sem("drows_ready", ctx)
            copied = sem("weights_copied", ctx)
            block = blocks.enter_context(nc.Block())
            loads = []

            def column(v):
                return v.rearrange("(f a) -> f a", a=1)

            loads += [(W["W1l"][:, :], a["L0_gnn_W1_l"]), (W["W1r"][:, :], a["L0_gnn_W1_r"]),
                      (W["W2l"][:, :], a["L0_gnn_W2_l"]), (W["W2r"][:, :], a["L0_gnn_W2_r"])]
            loads += [(raw[n][:, :], a["L1_gnn_" + n]) for n in raw]
            loads += [(rawS[:, 2:6], a["L1_gnn_WS"]), (rawe1[:, :], a["L1_gnn_se_w1"]), (rawe2[:, :], a["L1_gnn_se_w2"]),
                      (raw1[:, :, :], a["L1_gnn_ffn_w1"].rearrange("(c p) n -> p c n", p=P)), (raw2[:, :], a["L1_gnn_ffn_w2"])]
            loads += [(col["b1"][:, :], column(a["L0_gnn_b1"])), (col["b2"][:, :], column(a["L0_gnn_b2"])),
                      (col["a1"][:, :], a["L0_gnn_att1"].rearrange("h (c a) -> (h c) a", a=1)),
                      (col["a2"][:, :], a["L0_gnn_att2"].rearrange("h (c a) -> (h c) a", a=1)),
                      (seb1[:, :], column(a["L1_gnn_se_b1"])),
                      (fb1[:, :], a["L1_gnn_ffn_b1"].rearrange("(c p) -> p c", p=P))]
            loads += [(col[n][:, :], column(a["L1_gnn_" + n])) for n in ("ln1_g", "ln1_b", "ln2_g", "ln2_b", "w_a", "ffn_b2", "se_b2")]
            loads += [(row["b1"][:, :], a["L0_gnn_b1"].partition_broadcast(P)), (row["b2"][:, :], a["L0_gnn_b2"].partition_broadcast(P)),
                      (row["w_g"][:, :], a["L1_gnn_w_g"].partition_broadcast(P)), (row["b_g"][:, :], a["L1_gnn_b_g"].partition_broadcast(P))]
            loads += [(WG6[0:1, :], a["L1_gnn_w_g"].partition_broadcast(1)), (WG6[1:2, :], a["L1_gnn_b_g"].partition_broadcast(1))]

            @block.sync
            def _(sp):
                dst2 = a["dst"].rearrange("(p t) -> p t", t=T)
                sp.wait_ge(pads, 3)
                sp.dma_start(dint[:, 1:T + 1], dst2).then_inc(edges_in, 16)
                sp.dma_start(dint[1:EP, 0:1], dst2[0:EP - 1, T - 1:T], allow_slow_non_contiguous=True).then_inc(edges_in, 16)
                sp.dma_start(dint[0:EP - 1, T + 1:T + 2], dst2[1:EP, 0:1], allow_slow_non_contiguous=True).then_inc(edges_in, 16)
                sp.dma_start(sint[:, :], a["src"].rearrange("(p t) -> p t", t=T)).then_inc(edges_in, 16)
                sp.wait_ge(pads, 3)
                for to, of in loads:
                    sp.dma_start(to, of, allow_slow_non_contiguous=True).then_inc(loaded, 16)

            @block.gpsimd
            def _(pool):
                pool.memset(dint[:, :], -1).then_inc(pads, 1)
                pool.memset(WG6[:, :], 0.0).then_inc(pads, 1)
                pool.memset(rawS[:, :], 0.0).then_inc(pads, 1)
                c = Chain(pool, madeg)
                c.put(pool.memset(ident[:, :], 0.0))
                c.put(pool.memset(ones[:, :], 1.0))
                c.put(pool.memset(tail_ones[:, :], 1.0))
                c.put(pool.memset(headmask[:, :], 1.0))
                c.put(pool.memset(half[:, :], -0.5))
                c.sync()
                c.put(pool.affine_select(out=ident[:, :], in_=ident[:, :], compare_op=ALU.not_equal, fill=1.0,
                                         base=0, pattern=[[-1, P]], channel_multiplier=1))
                c.put(pool.affine_select(out=tail_ones[:, :], in_=tail_ones[:, :], compare_op=ALU.is_ge, fill=0.0,
                                         base=-(GROUP - TAIL), pattern=[[0, 1]], channel_multiplier=J))
                c.put(pool.affine_select(out=headmask[:, :], in_=headmask[:, :], compare_op=ALU.is_ge, fill=0.0,
                                         base=0, pattern=[[-32, 4]], channel_multiplier=1))
                c.sync()
                c.put(pool.affine_select(out=headmask[:, :], in_=headmask[:, :], compare_op=ALU.is_ge, fill=0.0,
                                         base=31, pattern=[[32, 4]], channel_multiplier=-1))
                c.sync()
                pool.sem_inc(made, 1)

            @block.tensor
            def _(pe):
                pe.wait_ge(made, 1)
                pe.wait_ge(loaded, 16 * len(loads))
                idt = ident[:, :]
                for i, n in enumerate(("WQ", "WK", "WV", "WE")):
                    nc.tensor.transpose(ps[0][:, i * P:(i + 1) * P], raw[n][:, :], idt)
                for i in range(4):
                    nc.tensor.transpose(ps[1][:, i * P:(i + 1) * P], raw1[:, i, :], idt)
                    nc.tensor.transpose(ps[2][:, i * P:(i + 1) * P], raw2[:, i * P:(i + 1) * P], idt)
                nc.tensor.transpose(ps[3][0:6, 0:P], rawS[:, :], idt)
                nc.tensor.transpose(ps[3][:, P:P + 32], rawe1[:, :], ident[0:32, 0:32])
                nc.tensor.transpose(ps[3][0:32, 2 * P:3 * P], rawe2[:, :], idt).then_inc(turned, 1)
                pe.wait_ge(diag, 1)
                for i in range(2):
                    last = nc.tensor.matmul(ps[4][0:EP, i * EP:(i + 1) * EP], ones[0:EP, 0:EP], dg[:, i, :], start=True, stop=True)
                last.then_inc(drows, 1)

            @block.scalar
            def _(act):
                act.wait_ge(turned, 1)
                for i, n in enumerate(("WQT", "WKT", "WVT", "WET")):
                    act.activation(W[n][:, :], ps[0][:, i * P:(i + 1) * P], ACT.Copy)
                act.activation(F1T[:, :, :], ps[1][:, :].rearrange("p (c n) -> p c n", c=4), ACT.Copy)
                act.activation(F2T[:, :, :], ps[2][:, :].rearrange("p (c n) -> p c n", c=4), ACT.Copy)
                act.activation(WS6[:, :], ps[3][0:6, 0:P], ACT.Copy)
                act.activation(S1T[:, :], ps[3][:, P:P + 32], ACT.Copy)
                act.activation(S2T[:, :], ps[3][0:32, 2 * P:3 * P], ACT.Copy).then_inc(copied, 1)
                act.wait_ge(copied, 1)

            @block.vector
            def _(v):
                c = Chain(v, vec)
                v.wait_ge(made, 1)
                v.wait_ge(loaded, 16 * len(loads))
                for i, n in enumerate(("a1", "a2")):
                    c.put(v.tensor_scalar(att[i][:, 0:4], headmask[:, :], col[n][:, :], None, ALU.mult))
                    c.put(v.tensor_scalar(att[i][:, 4:8], headmask[:, :], col[n][:, :], -0.2, ALU.mult, ALU.mult))
                v.wait_ge(edges_in, 64)
                c.put(v.tensor_copy(d[:, :], dint[:, :]))
                c.put(v.tensor_copy(idx[:, :, 0], sint[:, :]))
                c.put(v.tensor_copy(idx[:, :, 1], dint[:, 1:T + 1]))
                c.put(v.tensor_scalar(idx[:, :, 2], sint[:, :], 2.0, None, ALU.mult))
                c.put(v.tensor_copy(idx[:, :, 3], dint[:, 1:T + 1]))
                c.sync()
                now = d[:, 1:T + 1]
                c.put(v.tensor_tensor(stt[:, :], now, d[:, 0:T], ALU.not_equal))
                c.put(v.tensor_tensor(ent[:, :], now, d[:, 2:T + 2], ALU.not_equal))
                c.put(v.tensor_scalar(dg[:, 0, :], ident[0:EP, 0:EP], d[:, T:T + 1], None, ALU.mult))
                c.put(v.tensor_scalar(dg[:, 1, :], ident[0:EP, 0:EP], d[:, 1:2], None, ALU.mult))
                c.sync()
                c.put(v.tensor_scalar(sm[:, 0:1], stt[:, 0:1], -1.0, 1.0, ALU.mult, ALU.add))
                v.sem_inc(diag, 1)
                c.sync()
                c.put(v.tensor_scalar(hrt[:, :], now, d[:, 1:2], sm[:, 0:1], ALU.is_equal, ALU.mult))
                c.put(v.tensor_scalar(flag[:, :, 1], stt[:, :], 1.0, -NEG, ALU.subtract, ALU.mult))
                c.put(v.tensor_scalar(flag[:, :, 0], stt[:, :], NEG, None, ALU.mult))
                c.sync()
                c.put(v.memset(flag[:, 0, 0:1], NEG))
                c.put(v.tensor_tensor(het[:, :], hrt[:, :], ent[:, :], ALU.mult))
                c.sync()
                c.put(v.tensor_tensor(wrt[:, :], ent[:, :], het[:, :], ALU.subtract))
                c.sync()
                c.put(v.memset(het[:, T - 1:T], 0.0))
                c.put(v.memset(wrt[:, T - 1:T], 0.0))
                c.sync()
                c.put(v.tensor_copy(flag[:, :, 2], het[:, :]))
                c.put(v.tensor_scalar(tmp[:, :], wrt[:, :], -SKIP, SKIP, ALU.mult, ALU.add))
                c.put(v.tensor_reduce(sm[:, 1:2], het[:, :], AX.X, ALU.max))
                c.sync()
                c.put(v.tensor_tensor(idx[:, :, 4], tmp[:, :], now, ALU.add))
                c.put(v.tensor_scalar(sm[:, 2:3], sm[:, 1:2], -SKIP, SKIP, ALU.mult, ALU.add))
                c.put(v.tensor_scalar(sm[:, 3:4], ent[:, T - 1:T], -SKIP, SKIP, ALU.mult, ALU.add))
                c.sync()
                c.put(v.tensor_tensor(idxP[:, 0:1], sm[:, 3:4], d[:, T:T + 1], ALU.add))
                c.put(v.tensor_tensor(idxP[:, 1:2], sm[:, 2:3], d[:, 1:2], ALU.add))
                v.wait_ge(drows, 1)
                c.put(v.tensor_copy(drow[:, :, :], ps[4][0:EP, 0:2 * EP].rearrange("p (a q) -> p a q", a=2)))
                c.sync()
                c.put(v.tensor_scalar(ET[:, :], drow[:, 0, :], d[:, T:T + 1], None, ALU.is_equal))
                c.put(v.tensor_scalar(EA[:, :], drow[:, 1, :], d[:, T:T + 1], None, ALU.is_equal))
                c.put(v.tensor_scalar(EB[:, :], drow[:, 0, :], d[:, 1:2], None, ALU.is_equal))
                c.sync()
                c.put(v.tensor_scalar(NT[:, :], ET[:, :], 1.0, -NEG, ALU.subtract, ALU.mult))
                c.put(v.tensor_scalar(NBm[:, :], EB[:, :], 1.0, -NEG, ALU.subtract, ALU.mult))
                c.sync()

            blocks.close()
            clear_semaphores(nc, used)
            used.clear()

        with ExitStack() as ctx, ExitStack() as blocks:
            X = sb("X", [P, 2 * SLOTS, J, 2 * P], ctx=ctx)
            H1N = sb("H1N", [P, SLOTS, J, P], ctx=ctx)
            X1 = sb("X1", [P, SLOTS, J, P], ctx=ctx)
            bn = sb("bn", [P, SLOTS, J, 6], ctx=ctx)
            mean = sb("mean", [P, SLOTS, J], ctx=ctx)
            vpe = sb("vpe", [P, SLOTS, J], ctx=ctx)
            tmpm = sb("tmpm", [P, 3, J], ctx=ctx)
            rstd = sb("rstd", [P, SLOTS, J], ctx=ctx)
            h0T, h1T, h2T = (sb(n, [P, 2, GROUP], ctx=ctx) for n in ("h0T", "h1T", "h2T"))
            pT0, pM1, pM2, pN1, pN2 = (pb(n, ctx) for n in ("pT0", "pM1", "pM2", "pN1", "pN2"))
            x_in = [sem(f"x_in{s}", ctx) for s in range(2 * SLOTS)]
            xx_out = [sem(f"xx_out{s}", ctx) for s in range(2 * SLOTS)]
            h1_out = [sem(f"h1_out{s}", ctx) for s in range(SLOTS)]
            x1_out = [sem(f"x1_out{s}", ctx) for s in range(SLOTS)]
            K_TAKE = J + 7
            names = ("moments_steps", "rstd_ready", "xn_ready", "x1_ready", "tr0", "mm1", "mm2", "tr1", "tr2",
                     "h0T_ready", "h1T_ready", "h1N_ready", "h2T_ready")
            (moments_steps, rstd_ready, xn_ready, x1_ready, tr0, mm1, mm2, tr1, tr2,
             h0T_ready, h1T_ready, h1N_ready, h2T_ready) = (sem(n, ctx) for n in names)
            block = blocks.enter_context(nc.Block())

            @block.sync
            def _(sp):
                def load(st):
                    need(sp, x1_ready, st.m - 7)
                    need(sp, xx_out[st.wslot], 16 * st.wk)
                    sp.dma_start(X[:, st.wslot, :, P:2 * P], rows_of(a["x"], st)).then_inc(x_in[st.wslot], 16)

                def store_xx(st):
                    sp.wait_ge(xn_ready, st.m + 1)
                    if st.last:
                        sp.wait_ge(xx_out[(st.m - 1) % (2 * SLOTS)], 16 * ((st.m - 1) // (2 * SLOTS) + 1))
                    sp.dma_start(rows_of(xx_t, st), X[:, st.wslot]).then_inc(xx_out[st.wslot], 16)

                def store(ready, buf, tab, done):
                    def fn(st):
                        sp.wait_ge(ready, st.m + 1)
                        if st.last:
                            sp.wait_ge(done[(st.m - 1) % SLOTS], 16 * ((st.m - 1) // SLOTS + 1))
                        sp.dma_start(rows_of(tab, st), buf[:, st.slot]).then_inc(done[st.slot], 16)
                    return fn

                run_steps(sp, NG, [(0, load), (2, store_xx), (4, store(h1N_ready, H1N, h1_t, h1_out)),
                                   (6, store(x1_ready, X1, x1_t, x1_out))], 2 * SLOTS)
                for done in (xx_out, h1_out, x1_out):
                    for s in range(len(done)):
                        sp.wait_ge(done[s], 16 * ((NG - 1 - s) // len(done) + 1))

            @block.gpsimd
            def _(pool):
                def rsqrt(st):
                    pool.wait_ge(moments_steps, (st.m + 1) * K_TAKE)
                    pool.tensor_tensor(rstd[:, st.slot], vpe[:, st.slot], half[:, 0:J], ALU.pow).then_inc(rstd_ready, 1)

                run_steps(pool, NG, [(0, rsqrt)])

            @block.vector
            def _(v):
                cm = Chain(v, moments_steps)

                def take_stats(st):
                    v.wait_ge(x_in[st.wslot], 16 * (st.wk + 1))
                    need(v, moments_steps, st.m * K_TAKE)
                    c = cm.at(st.m * K_TAKE)
                    for j in range(J):
                        c.put(v.bn_stats(bn[:, st.slot, j], X[:, st.wslot, j, P:2 * P]))
                    c.sync()
                    moments(v, c, bn[:, st.slot], mean[:, st.slot], vpe[:, st.slot], tmpm)
                    assert c.n == K_TAKE

                def normalise(st):
                    v.wait_ge(rstd_ready, st.m + 1)
                    need(v, tr0, st.m - 7)
                    for j in range(J):
                        last = v.tensor_scalar(X[:, st.wslot, j, 0:P], X[:, st.wslot, j, P:2 * P], mean[:, st.slot, j:j + 1],
                                               rstd[:, st.slot, j:j + 1], ALU.subtract, ALU.mult)
                    last.then_inc(xn_ready, 1)

                def residual(st):
                    v.wait_ge(tr2, st.m + 1)
                    need(v, x1_out[st.slot], 16 * st.k)
                    v.tensor_tensor(X1[:, st.slot], X[:, st.wslot, :, P:2 * P], pN2[:, :].rearrange("p (j f) -> p j f", j=J),
                                    ALU.add).then_inc(x1_ready, 1)

                run_steps(v, NG, [(1, normalise), (5, residual), (0, take_stats)], 2 * SLOTS)

            @block.tensor
            def _(pe):
                def turn_x(st):
                    pe.wait_ge(xn_ready, st.m + 1)
                    need(pe, h0T_ready, st.m)
                    for j in range(J):
                        last = nc.tensor.transpose(pT0[:, j * P:(j + 1) * P], X[:, st.wslot, j, 0:P], ident[:, :])
                    last.then_inc(tr0, 1)

                def layer1(st):
                    pe.wait_ge(h0T_ready, st.m + 1)
                    need(pe, h1T_ready, st.m)
                    nc.tensor.matmul(pM1[:, :], W["W1l"][:, :], h0T[:, st.slot % 2], start=True, stop=True).then_inc(mm1, 1)

                def layer2(st):
                    pe.wait_ge(h1T_ready, st.m + 1)
                    need(pe, h2T_ready, st.m)
                    nc.tensor.matmul(pM2[:, :], W["W2l"][:, :], h1T[:, st.slot % 2], start=True, stop=True).then_inc(mm2, 1)
                    need(pe, h1N_ready, st.m)
                    for j in range(J):
                        last = nc.tensor.transpose(pN1[:, j * P:(j + 1) * P], h1T[:, st.slot % 2, j * P:(j + 1) * P], ident[:, :])
                    last.then_inc(tr1, 1)

                def turn_h2(st):
                    pe.wait_ge(h2T_ready, st.m + 1)
                    need(pe, x1_ready, st.m)
                    for j in range(J):
                        last = nc.tensor.transpose(pN2[:, j * P:(j + 1) * P], h2T[:, st.slot % 2, j * P:(j + 1) * P], ident[:, :])
                    last.then_inc(tr2, 1)

                run_steps(pe, NG, [(0, turn_x), (3, turn_h2), (1, layer1), (2, layer2)], 2 * SLOTS)

            @block.scalar
            def _(act):
                def relu_x(st):
                    act.wait_ge(tr0, st.m + 1)
                    need(act, mm1, st.m - 1)
                    act.activation(h0T[:, st.slot % 2], pT0[:, :], ACT.Relu).then_inc(h0T_ready, 1)

                def relu_h1(st):
                    act.wait_ge(mm1, st.m + 1)
                    need(act, tr1, st.m - 1)
                    act.activation(h1T[:, st.slot % 2], pM1[:, :], ACT.Relu, bias=col["b1"][:, :]).then_inc(h1T_ready, 1)

                def copy_h1(st):
                    act.wait_ge(tr1, st.m + 1)
                    need(act, h1_out[st.slot], 16 * st.k)
                    act.activation(H1N[:, st.slot], pN1[:, :].rearrange("p (j f) -> p j f", j=J), ACT.Copy).then_inc(h1N_ready, 1)

                def relu_h2(st):
                    act.wait_ge(mm2, st.m + 1)
                    need(act, tr2, st.m - 1)
                    act.activation(h2T[:, st.slot % 2], pM2[:, :], ACT.Relu, bias=col["b2"][:, :]).then_inc(h2T_ready, 1)

                run_steps(act, NG, [(0, relu_x), (1, relu_h1), (2, relu_h2), (2, copy_h1)])

            blocks.close()
            clear_semaphores(nc, used)

        k = Shared()
        k.EA, k.ET, k.F1T, k.F2T, k.N, k.NB, k.NBm, k.NG, k.NT, k.S1T = EA, ET, F1T, F2T, N, NB, NBm, NG, NT, S1T
        k.S2T, k.T, k.W, k.WS6, k.ZR, k.a, k.col, k.fb1, k.flag, k.gsum = S2T, T, W, WS6, ZR, a, col, fb1, flag, gsum
        k.half, k.ident, k.idx, k.idxP, k.ones, k.row, k.rows_of, k.seb1, k.srow, k.tail_ones = half, ident, idx, idxP, ones, row, rows_of, seb1, srow, tail_ones
        k.WG6 = WG6
        k.x1_t, k.y2_t, k.z_rows, k.z_t, k.xe_t = x1_t, y2_t, z_rows, z_t, xe_t
        gat_layer(nc, k, 1, xx_t.rearrange("n (a f) -> (n a) f", a=2), xx_t, h1_t, None, W["W1l"], W["W1r"], att[0], row["b1"])
        gat_layer(nc, k, 2, h1_t, h1_t, x1_t, a["x"], W["W2l"], W["W2r"], att[1], row["b2"])
        edge_attention(nc, k)
        ffn_pass(nc, k)
        squeeze_and_out(nc, k)


_INS = ["x", "src", "dst", "L0_gnn_W1_l", "L0_gnn_W1_r", "L0_gnn_att1", "L0_gnn_b1", "L0_gnn_W2_l", "L0_gnn_W2_r", "L0_gnn_att2",
        "L0_gnn_b2", "L1_gnn_ln1_g", "L1_gnn_ln1_b", "L1_gnn_ln2_g", "L1_gnn_ln2_b", "L1_gnn_WQ", "L1_gnn_WK", "L1_gnn_WV",
        "L1_gnn_WS", "L1_gnn_WE", "L1_gnn_w_a", "L1_gnn_w_g", "L1_gnn_b_g", "L1_gnn_ffn_w1", "L1_gnn_ffn_b1", "L1_gnn_ffn_w2",
        "L1_gnn_ffn_b2", "L1_gnn_se_w1", "L1_gnn_se_b1", "L1_gnn_se_w2", "L1_gnn_se_b2"]


def kernel(**inputs):
    import numpy as _np
    import concourse.bacc as _bacc
    from concourse import mybir as _mybir
    from concourse.bass_utils import run_bass_kernel_spmd as _run

    nc = _bacc.Bacc("TRN2", target_bir_lowering=False, num_devices=1)
    arrays, args = {}, {}
    for name in _INS:
        v = _np.ascontiguousarray(inputs[name])
        arrays[f"in_{name}"] = v
        args[name] = nc.dram_tensor(f"in_{name}", v.shape, _mybir.dt.from_np(v.dtype), kind="ExternalInput").ap()
    n, e = inputs["x"].shape[0], inputs["src"].shape[0]
    args["out"] = nc.dram_tensor("out_0", (n, P), _mybir.dt.float32, kind="ExternalOutput").ap()
    build(nc, n, e, args)
    r = _run(nc, [arrays], core_ids=[0])
    return r.results[0]["out_0"]
```

```python
from contextlib import ExitStack

import concourse.bass as bass
from concourse import mybir
from concourse.alu_op_type import AluOpType as ALU

F32 = mybir.dt.float32
I32 = mybir.dt.int32
ACT = mybir.ActivationFunctionType
AX = mybir.AxisListType

P = 128
J = 4
GROUP = P * J
EP = 125
B = 4
SLOTS = 4
NEG = -1.0e30
SKIP = 4.0e6
EPS = 1.0e-5


class Step:

    def __init__(self, m, k, wk, off, unroll, last):
        self.m, self.k, self.wk, self.last = m, k, wk, last
        self.slot, self.wslot = off % SLOTS, off % unroll
        self.first = isinstance(m, int) and m == 0


def run_steps(eng, count, stages, unroll=SLOTS):
    deepest = max(lag for lag, _ in stages)
    head = -(-deepest // unroll) * unroll + unroll
    turns = max(0, (count - 1 - head) // unroll)

    def straight(n):
        for lag, fn in stages:
            m = n - lag
            if 0 <= m < count:
                fn(Step(m, m // SLOTS, m // unroll, m, unroll, m == count - 1))

    if turns == 0:
        for n in range(count + deepest):
            straight(n)
        return
    for n in range(head):
        straight(n)
    with eng.Fori(0, turns) as i:
        for u in range(unroll):
            for lag, fn in stages:
                off = head + u - lag
                fn(Step(i * unroll + off, i * (unroll // SLOTS) + off // SLOTS, i + off // unroll, off, unroll, False))
    for n in range(head + turns * unroll, count + deepest):
        straight(n)


def stand_alone(eng, passed):
    eng.sem_inc(passed, 1)


def need(eng, sem, value):
    if not (isinstance(value, int) and value <= 0):
        eng.wait_ge(sem, value)


def moments(v, c, bn, mean, vpe, tmp, sign=1.0, eps=None):
    m0, q0, m1, q1 = bn[:, :, 1], bn[:, :, 2], bn[:, :, 4], bn[:, :, 5]
    c.put(v.tensor_tensor(tmp[:, 0], m0, m1, ALU.add))
    c.put(v.tensor_tensor(tmp[:, 1], m0, m1, ALU.subtract))
    c.put(v.tensor_tensor(tmp[:, 2], q0, q1, ALU.add))
    c.sync()
    c.put(v.tensor_scalar(mean, tmp[:, 0], 0.5 * sign, None, ALU.mult))
    c.put(v.tensor_tensor(tmp[:, 1], tmp[:, 1], tmp[:, 1], ALU.mult))
    c.sync()
    c.put(v.scalar_tensor_tensor(tmp[:, 2], tmp[:, 1], P / 4.0, tmp[:, 2], ALU.mult, ALU.add))
    c.sync()
    if eps is None:
        c.put(v.tensor_scalar(vpe, tmp[:, 2], 1.0 / P, EPS, ALU.mult, ALU.add))
    else:
        c.put(v.scalar_tensor_tensor(vpe, tmp[:, 2], 1.0 / P, eps, ALU.mult, ALU.add))


def clear_semaphores(nc, sems):
    nums = sorted(x.num for x in sems)
    starts = [n for n in nums if n - 1 not in nums]
    with nc.Block() as block:
        @block.sync
        def _(sp):
            for n in starts:
                end = n
                while end in nums:
                    end += 1
                sp.sem_clear(range(n, end))


class Chain:

    def __init__(self, eng, sem):
        self.eng, self.sem, self.base, self.n = eng, sem, 0, 0

    def at(self, base):
        self.base, self.n = base, 0
        return self

    def put(self, ins):
        self.n += 1
        return ins.then_inc(self.sem, 1)

    def sync(self):
        self.eng.wait_ge(self.sem, self.base + self.n)


def join_pieces(nc, k, tag, H, C, state, F, ctx, sem, after_steps, finish, back=False):
    HW = H * (C + 1)
    same, cross, no_same, no_cross, idxP = (k.EF, k.EB, k.NF, k.NA, k.idxQ) if back else (k.ET, k.EA, k.NT, k.NBm, k.idxP)
    dgm, m1, m2 = (ctx.enter_context(nc.sbuf_tensor(tag + n, [EP, H, EP], F32)) for n in ("j_diag", "j_m1", "j_m2"))
    G, Q, QE = (ctx.enter_context(nc.sbuf_tensor(tag + n, [EP, 3 * H], F32)) for n in ("j_max", "j_arg", "j_exp"))
    TS, f1, f2 = (ctx.enter_context(nc.sbuf_tensor(tag + n, [EP, HW], F32)) for n in ("j_scaled", "j_f1", "j_f2"))
    FX = ctx.enter_context(nc.sbuf_tensor(tag + "j_total", [EP, 2, HW], F32))
    j_vec, j_diag, j_max, j_arg, j_exp, j_scaled, j_sum, j_rows = (
        sem(n) for n in ("j_vec", "j_diag_ready", "j_max_ready", "j_arg_ready", "j_exp_ready", "j_scaled_ready", "j_sum_ready", "j_rows_ready"))
    T_ = state

    def heads(ap):
        return ap.rearrange("p (h c) -> p h c", h=H)

    def over(ap, n):
        return ap.unsqueeze(2).to_broadcast([EP, H, n])

    def vec(v, out):
        c = Chain(v, j_vec)
        v.wait_ge(*after_steps)
        for h in range(H):
            c.put(v.tensor_scalar(dgm[:, h], k.ident[0:EP, 0:EP], T_[:, HW + h:HW + h + 1], None, ALU.mult))
        c.sync()
        v.sem_inc(j_diag, 1)
        v.wait_ge(j_max, 1)
        rows = k.join_ps[0][0:EP, 0:H * EP].rearrange("p (h q) -> p h q", h=H)
        c.put(v.tensor_tensor(m1[:, :, :], rows, no_same[:, :].unsqueeze(1).to_broadcast([EP, H, EP]), ALU.add))
        c.put(v.tensor_tensor(m2[:, :, :], rows, no_cross[:, :].unsqueeze(1).to_broadcast([EP, H, EP]), ALU.add))
        c.sync()
        c.put(v.tensor_reduce(G[:, 0:H], m1[:, :, :], AX.X, ALU.max))
        c.put(v.tensor_reduce(G[:, H:2 * H], m2[:, :, :], AX.X, ALU.max))
        c.sync()
        c.put(v.tensor_tensor(G[:, 2 * H:3 * H], F[:, HW:HW + H], G[:, H:2 * H], ALU.max))
        c.put(v.tensor_tensor(Q[:, 0:H], T_[:, HW:HW + H], G[:, 0:H], ALU.subtract))
        c.sync()
        c.put(v.tensor_tensor(Q[:, H:2 * H], F[:, HW:HW + H], G[:, 2 * H:3 * H], ALU.subtract))
        c.put(v.tensor_tensor(Q[:, 2 * H:3 * H], G[:, H:2 * H], G[:, 2 * H:3 * H], ALU.subtract))
        c.sync()
        v.sem_inc(j_arg, 1)
        v.wait_ge(j_exp, 1)
        c.put(v.tensor_tensor(heads(TS[:, :]), heads(T_[:, 0:HW]), over(QE[:, 0:H], C + 1), ALU.mult))
        c.put(v.tensor_tensor(heads(f1[:, :]), heads(F[:, 0:HW]), over(QE[:, H:2 * H], C + 1), ALU.mult))
        c.sync()
        v.sem_inc(j_scaled, 1)
        v.wait_ge(j_sum, 1)
        c.put(v.tensor_copy(FX[:, 0], k.join_ps[1][0:EP, 0:HW]))
        c.put(v.tensor_tensor(heads(f2[:, :]), heads(k.join_ps[1][0:EP, 256:256 + HW]), over(QE[:, 2 * H:3 * H], C + 1), ALU.mult))
        c.sync()
        c.put(v.tensor_tensor(FX[:, 1], f1[:, :], f2[:, :], ALU.add))
        c.sync()
        finish(v, c, FX[:, :, :].rearrange("p n (h c) -> p n h c", h=H), 2, out)
        c.sync()
        v.sem_inc(j_rows, 1)

    def pe(_):
        nc.tensor.wait_ge(j_diag, 1)
        for h in range(H):
            last = nc.tensor.matmul(k.join_ps[0][0:EP, h * EP:(h + 1) * EP], k.ones[0:EP, 0:EP], dgm[:, h], start=True, stop=True)
        last.then_inc(j_max, 1)
        nc.tensor.wait_ge(j_scaled, 1)
        nc.tensor.matmul(k.join_ps[1][0:EP, 0:HW], same[:, :], TS[:, :], start=True, stop=True)
        nc.tensor.matmul(k.join_ps[1][0:EP, 256:256 + HW], cross[:, :], TS[:, :], start=True, stop=True).then_inc(j_sum, 1)

    def act(act_):
        act_.wait_ge(j_arg, 1)
        act_.activation(QE[:, :], Q[:, :], ACT.Exp).then_inc(j_exp, 1)

    def pool(pool_, out, table, done, last_row):
        pool_.wait_ge(j_rows, 1)
        for n in range(2):
            pool_.indirect_dma_start(table, bass.IndirectOffsetOnAxis(idxP[:, n:n + 1], 0), out[:, n], None,
                                     bounds_check=last_row, oob_is_err=False).then_inc(done, 16)
        pool_.wait_ge(done, 32)

    return vec, pe, act, pool


def mask_rows(act, rows, keep):
    for t in range(B):
        last = act.activation(rows[:, t], rows[:, t], ACT.Copy, scale=keep[:, t, 0:1])
    return last


def carry_rows(v, c, to, rows, keep, order):
    for t, before in order:
        c.put(v.scalar_tensor_tensor(to(t), before, keep[:, t, 1:2], rows[:, t], ALU.mult, ALU.add))
        c.sync()


def gather(pool, to, table, index, last_row):
    return pool.indirect_dma_start(to, None, table, bass.IndirectOffsetOnAxis(index, 0), bounds_check=last_row, oob_is_err=False)


def gat_layer(nc, k, layer, src_t, dst_t, out_t, res_t, Wl, Wr, attc, brow):
    back = layer == 2
    order = list(range(B))[::-1] if back else list(range(B))
    own, old = (0, 1) if back else (1, 0)
    end = 0 if back else B
    begin = B - end
    H, C = 4, 32
    HW = H * (C + 1)
    HS = HW + H
    T, NB, N = k.T, k.NB, k.N
    first_flag = 5 if back else 2
    K_ARGS = 7 + B
    K_MAIN = 4 + 2 * B + (3 if back else 5)
    used = []
    with ExitStack() as ctx, ExitStack() as blocks:
        def sb(name, shape, dt=F32):
            return ctx.enter_context(nc.sbuf_tensor(f"g{layer}_{name}", list(shape), dt))

        def sem(name):
            if name.rstrip("0123") in k.by_pool_dma:
                return k.whole.enter_context(nc.semaphore(f"{name}_{layer}"))
            used.append(ctx.enter_context(nc.semaphore(f"{name}_{layer}")))
            return used[-1]

        IB = sb("IB", [EP, SLOTS, B, 2], I32)
        OB = sb("OB", [EP, SLOTS, B], I32)
        FB = sb("FB", [EP, SLOTS, B, 3])
        KF = sb("KF", [EP, SLOTS, B, 2]) if back else None
        DR = sb("DR", [EP, SLOTS, B, P]) if back else None
        ends = sb("ends", [EP, 2, P])
        DW = 2 * P if layer == 1 else P
        XS, XD = sb("XS", [EP, SLOTS, B, P]), sb("XD", [EP, SLOTS, B, DW])
        XR = sb("XR", [EP, SLOTS, B, P]) if res_t is not None else None
        sdT = sb("sdT", [P, SLOTS, 2, B * EP])
        lr = sb("lr", [P, 2, 2, B * EP])
        EM = sb("EM", [EP, SLOTS, B, H])
        D1 = sb("D1", [EP, SLOTS, B, H])
        MH = sb("MH", [EP, SLOTS, B + 1, H])
        CB = sb("CB", [EP, SLOTS, B, H])
        A = sb("A", [EP, SLOTS, B, 3 * H])
        XE = sb("XE", [EP, SLOTS, B, 3 * H])
        Wt = sb("Wt", [EP, 2, B, HW])
        W2 = sb("W2", [EP, 2, B, P])
        prod = sb("prod", [EP, HW])
        ST = sb("ST", [EP, SLOTS, B, HS])
        TF = sb("TF", [EP, 2, B, HS])
        F = sb("F", [EP, HS])
        den = sb("den", [EP, 2, B, H])
        O = sb("O", [EP, SLOTS, B, P])
        OJ, XJ = sb("OJ", [EP, 2, P]), sb("XJ", [EP, 2, P])
        zero = sb("zero", [P, k.ZR]) if layer == 1 else None
        pTs, pTd, pS, pD, pV, pU, pL, pF = (ctx.enter_context(nc.psum_tensor(f"g{layer}_{n}", [P, 512], F32))
                                        for n in ("pTs", "pTd", "pS", "pD", "pV", "pU", "pL", "pF"))
        gat = [sem(f"gat{s}") for s in range(SLOTS)]
        rows_out = [sem(f"rows_out{s}") for s in range(SLOTS)]
        idx_in, flags_in, tr_done, sdT_ready, mm_done, v_done, lr_ready, lg_done, exp_done, args_steps, main_steps, init, join_in, join_out, clr, zero_made, passed = (
            sem(n) for n in ("idx_in", "flags_in", "tr_done", "sdT_ready", "mm_done", "v_done", "lr_ready", "lg_done", "exp_done",
                             "args_steps", "main_steps", "init", "join_in", "join_out", "z_cleared", "zero_made", "passed"))
        gathers = B if back else 2 * B
        dr_out = [sem(f"dr_out{s}") for s in range(SLOTS)]
        dr_in = [sem(f"dr_in{s}") for s in range(SLOTS)] if back else None
        fifth_ready, piece_ready, piece_done, piece_in = (sem(n) for n in ("fifth_ready", "piece_ready", "piece_done", "piece_in"))
        masked, bias_in, x_added = (sem(n) for n in ("masked", "bias_in", "x_added")) if back else (None, None, None)
        ends_in, ends_out, ends_scattered, keep_in, carry_steps = (sem(n) for n in ("ends_in", "ends_out", "ends_scattered", "keep_in", "carry_steps"))
        K_CARRY = B
        rows_to = k.dst_rows[layer - 1].rearrange("(p t) f -> p t f", t=T)
        rows_from = k.dst_rows[0].rearrange("(p t) f -> p t f", t=T)
        xe_rows = k.xe_t.rearrange("(p t) f -> p t f", t=T)
        xe = [sem(f"xe{s}") for s in range(SLOTS)]
        k.join_ps = (pS, pD)

        def rows_ready(eng, st):
            if back:
                eng.wait_ge(x_added, st.m + 1)
            else:
                eng.wait_ge(main_steps, (st.m + 1) * K_MAIN)

        def steps(st):
            return bass.ds(st.m * -B + (NB - 1) * B, B) if back else bass.ds(st.m * B, B)

        def heads(ap):
            return ap.rearrange("p t (h c) -> p t h c", h=H)

        def over(ap, n):
            return ap.unsqueeze(3).to_broadcast([EP, B, H, n])

        def finish(v, c, acc, n, out, dn, xr, split=False):
            c.put(v.tensor_scalar(dn, acc[:, :, :, C], 1e-16, None, ALU.add))
            c.sync()
            c.put(v.reciprocal(dn, dn))
            c.sync()
            c.put(v.tensor_tensor(out.rearrange("p t (h c) -> p t h c", h=H), acc[:, :, :, 0:C],
                                  dn.unsqueeze(3).to_broadcast([EP, n, H, C]), ALU.mult))
            if split:
                return
            c.sync()
            c.put(v.tensor_tensor(out, out, brow[0:EP, :].unsqueeze(1).to_broadcast([EP, n, P]), ALU.add))
            c.sync()
            if xr is None:
                c.put(v.tensor_scalar(out, out, 0.0, None, ALU.max))
            else:
                c.put(v.scalar_tensor_tensor(out, out, 0.0, xr, ALU.max, ALU.add))

        join_vec, join_pe, join_act, join_pool = join_pieces(
            nc, k, f"g{layer}_", H, C, ST[:, (NB - 1) % SLOTS, order[-1]], F, ctx, sem, (main_steps, NB * K_MAIN),
            lambda v, c, acc, n, out: finish(v, c, acc, n, out, den[:, 0, 0:2], XJ[:, :, :] if res_t is not None else None), back)
        block = blocks.enter_context(nc.Block())

        @block.sync
        def _(sp):
            def clear_z(st):
                sp.dma_start(k.z_t[bass.ds(st.m * k.ZR, k.ZR), :].rearrange("(p j) f -> p (j f)", p=P), zero[:, :]).then_inc(clr, 16)

            def keep_x(st):
                sp.wait_ge(gat[st.slot], 16 * gathers * (st.k + 1))
                sp.dma_start(xe_rows[:, steps(st), :], XD[:, st.slot, :, P:2 * P]).then_inc(xe[st.slot], 16)

            def load_x(st):
                need(sp, x_added, st.m - 3)
                sp.dma_start(XR[:, st.slot], xe_rows[:, steps(st), :]).then_inc(xe[st.slot], 16)

            def load_rows(st):
                need(sp, carry_steps, (st.m - 3) * K_CARRY)
                sp.dma_start(DR[:, st.slot], rows_from[:, steps(st), :]).then_inc(dr_in[st.slot], 16)

            def store_rows(st):
                rows_ready(sp, st)
                sp.dma_start(rows_to[:, steps(st), :], O[:, st.slot]).then_inc(dr_out[st.slot], 16)

            if zero is not None:
                sp.wait_ge(zero_made, 1)
            run_steps(sp, NB, ([(0, load_rows), (0, load_x)] if back else [(0, keep_x), (0, clear_z)]) + [(5 if back else 4, store_rows)])
            for s in range(SLOTS):
                sp.wait_ge(dr_out[s], 16 * ((NB - 1 - s) // SLOTS + 1))
            sp.wait_ge(ends_in, 32)
            edge = 0 if back else T - 1
            sp.dma_start(rows_to[:, edge, :], ends[:, 0], allow_slow_non_contiguous=True).then_inc(ends_out, 16)
            sp.wait_ge(ends_out, 16)
            if zero is not None:
                sp.wait_ge(clr, 16 * NB)
            for s in range(SLOTS):
                sp.wait_ge(xe[s], 16 * ((NB - 1 - s) // SLOTS + 1))

        @block.gpsimd
        def _(pool):
            if zero is not None:
                pool.memset(zero[:, :], 0.0).then_inc(zero_made, 1)

            last_row = pool.to_reg(N - 1)
            last_source = pool.to_reg(2 * N - 1) if layer == 1 else last_row

            def fetch(st):
                s = st.slot
                need(pool, gat[s], 16 * gathers * st.k)
                pool.tensor_copy(IB[:, s], k.idx[:, steps(st), (2 if layer == 1 else 0):(4 if layer == 1 else 2)]).then_inc(idx_in, 1)
                if back:
                    need(pool, carry_steps, (st.m - 3) * K_CARRY)
                    pool.tensor_copy(KF[:, s], k.flag[:, steps(st), 8:10]).then_inc(keep_in, 1)
                pool.wait_ge(idx_in, st.m + 1)
                need(pool, tr_done, st.m - 3)
                if layer == 1:
                    need(pool, xe[s], 16 * st.k)
                stand_alone(pool, passed)
                for t in range(B):
                    gather(pool, XS[:, s, t], src_t, IB[:, s, t, 0:1], last_source).then_inc(gat[s], 16)
                    if not back:
                        gather(pool, XD[:, s, t], dst_t, IB[:, s, t, 1:2], last_row).then_inc(gat[s], 16)

            def flags(st):
                s = st.slot
                need(pool, rows_out[s], 16 * B * st.k)
                pool.tensor_copy(OB[:, s], k.idx[:, steps(st), 5 if back else 4])
                need(pool, piece_ready, st.m - 3)
                pool.tensor_copy(FB[:, s], k.flag[:, steps(st), first_flag:first_flag + 3]).then_inc(flags_in, 1)

            def write_rows(st):
                pool.wait_ge(flags_in, st.m + 1)
                rows_ready(pool, st)
                stand_alone(pool, passed)
                for t in range(B):
                    pool.indirect_dma_start(out_t, bass.IndirectOffsetOnAxis(OB[:, st.slot, t:t + 1], 0), O[:, st.slot, t], None,
                                            bounds_check=last_row, oob_is_err=False).then_inc(rows_out[st.slot], 16)

            def add_bias(st):
                pool.wait_ge(main_steps, (st.m + 1) * K_MAIN)
                pool.tensor_tensor(O[:, st.slot], O[:, st.slot], brow[0:EP, :].unsqueeze(1).to_broadcast([EP, B, P]), ALU.add).then_inc(bias_in, 1)

            run_steps(pool, NB, [(4, add_bias), (5, write_rows), (0, fetch), (1, flags)] if back else
                      [(0, fetch), (1, flags), (4, write_rows)])
            if res_t is not None:
                gather(pool, XJ[:, 0], res_t, k.idx[:, 0, 1:2], last_row).then_inc(join_in, 16)
                gather(pool, XJ[:, 1], res_t, k.idx[:, T - 1, 1:2], last_row).then_inc(join_in, 16)
            join_pool(pool, OJ, out_t, join_out, last_row)
            for s in range(SLOTS):
                pool.wait_ge(rows_out[s], 16 * B * ((NB - 1 - s) // SLOTS + 1))
                pool.wait_ge(dr_out[s], 16 * ((NB - 1 - s) // SLOTS + 1))
            for n, t in enumerate((0, T - 1) if back else (T - 1, 0)):
                gather(pool, ends[:, n], out_t, k.idx[:, t, 1:2], last_row).then_inc(ends_in, 16)
            pool.wait_ge(ends_in, 32)
            pool.indirect_dma_start(k.dst_rows[layer - 1][:, :], bass.IndirectOffsetOnAxis(k.idxE[:, layer - 1:layer], 0), ends[:, 1], None,
                                    bounds_check=pool.to_reg(k.E - 1), oob_is_err=False).then_inc(ends_scattered, 16)
            pool.wait_ge(ends_scattered, 16)

        @block.tensor
        def _(pe):
            def turn(st):
                s = st.slot
                pe.wait_ge(gat[s], 16 * gathers * (st.k + 1))
                if back:
                    pe.wait_ge(carry_steps, (st.m + 1) * K_CARRY)
                need(pe, sdT_ready, st.m)
                for to, rows in ((pTs, XS), (pTd, XD[:, :, :, 0:P])):
                    for t in range(B):
                        last = nc.tensor.transpose(to[:, t * EP:(t + 1) * EP], rows[:, s, t], k.ident[0:EP, 0:EP])
                last.then_inc(tr_done, 1)

            def project(st):
                pe.wait_ge(sdT_ready, st.m + 1)
                need(pe, lr_ready, st.m)
                sT, dT = sdT[:, st.slot, 0], sdT[:, st.slot, 1]
                nc.tensor.matmul(pS[:, 0:B * EP], Wl[:, :], sT, start=True, stop=False)
                nc.tensor.matmul(pS[:, 0:B * EP], Wr[:, :], dT, start=False, stop=True)
                nc.tensor.matmul(pD[:, 0:B * EP], Wl[:, :], dT, start=True, stop=False)
                nc.tensor.matmul(pD[:, 0:B * EP], Wr[:, :], dT, start=False, stop=True).then_inc(mm_done, 1)

            def values(st):
                sT, dT = sdT[:, st.slot, 0], sdT[:, st.slot, 1]
                need(pe, main_steps, (st.m - 1) * K_MAIN + 3)
                for t in range(B):
                    nc.tensor.matmul(pV[0:EP, t * P:(t + 1) * P], sT[:, t * EP:(t + 1) * EP], Wl[:, :], start=True, stop=True)
                    last = nc.tensor.matmul(pU[0:EP, t * P:(t + 1) * P], dT[:, t * EP:(t + 1) * EP], Wl[:, :], start=True, stop=True)
                last.then_inc(v_done, 1)

            def logits(st):
                p = st.slot % 2
                pe.wait_ge(lr_ready, st.m + 1)
                need(pe, args_steps, st.m * K_ARGS)
                for t in range(B):
                    for i in range(2):
                        to = pL[0:EP, (2 * t + i) * H:(2 * t + i + 1) * H]
                        last = nc.tensor.matmul(to, lr[:, p, i, t * EP:(t + 1) * EP], attc[:, :], start=True, stop=True)
                last.then_inc(lg_done, 1)

            def keep_piece(st):
                pe.wait_ge(piece_ready, st.m + 1)
                for t in range(B):
                    last = nc.tensor.matmul(pF[0:EP, 0:HS], k.ident[0:EP, 0:EP], TF[:, st.slot % 2, t], start=st.first and t == 0, stop=st.last and t == B - 1)
                last.then_inc(piece_done, 1)

            run_steps(pe, NB, [(1, project), (2, logits), (2, values), (0, turn), (5, keep_piece)])
            join_pe(pe)

        @block.scalar
        def _(act):
            def relu_rows(st):
                act.wait_ge(tr_done, st.m + 1)
                need(act, v_done, st.m - 3)
                act.activation(sdT[:, st.slot, 0], pTs[:, 0:B * EP], ACT.Relu)
                act.activation(sdT[:, st.slot, 1], pTd[:, 0:B * EP], ACT.Relu).then_inc(sdT_ready, 1)

            def exps(st):
                act.wait_ge(args_steps, (st.m + 1) * K_ARGS)
                need(act, main_steps, (st.m - 3) * K_MAIN)
                act.activation(ST[:, st.slot, :, HW:HS], MH[:, st.slot, own:own + B], ACT.Copy)
                act.activation(XE[:, st.slot], A[:, st.slot], ACT.Exp).then_inc(exp_done, 1)

            def fifth(st):
                p = st.slot % 2
                act.wait_ge(mm_done, st.m + 1)
                need(act, lg_done, st.m - 1)
                for i, of in enumerate((pS, pD)):
                    last = act.activation(lr[:, p, i], of[:, 0:B * EP], ACT.Copy, scale=0.2)
                last.then_inc(fifth_ready, 1)

            def end_piece(st):
                act.wait_ge(main_steps, (st.m + 1) * K_MAIN)
                need(act, piece_done, st.m - 1)
                for t in range(B):
                    last = act.activation(TF[:, st.slot % 2, t], ST[:, st.slot, t], ACT.Copy, scale=FB[:, st.slot, t, 2:3])
                last.then_inc(piece_ready, 1)

            def mask(st):
                act.wait_ge(dr_in[st.slot], 16 * (st.k + 1))
                act.wait_ge(keep_in, st.m + 1)
                mask_rows(act, DR[:, st.slot], KF[:, st.slot]).then_inc(masked, 1)

            run_steps(act, NB, ([(0, mask)] if back else []) + [(1, fifth), (2, exps), (0, relu_rows), (4, end_piece)])
            join_act(act)

        @block.vector
        def _(v):
            v.memset(MH[:, SLOTS - 1], 0.0).then_inc(init, 1)
            v.memset(ST[:, SLOTS - 1], 0.0).then_inc(init, 1)
            if back:
                v.memset(XD[:, SLOTS - 1], 0.0).then_inc(init, 1)
            v.wait_ge(init, 3 if back else 2)
            ca, cm, ck = Chain(v, args_steps), Chain(v, main_steps), Chain(v, carry_steps)

            def carry(st):
                s, prev = st.slot, (st.slot - 1) % SLOTS
                v.wait_ge(masked, st.m + 1)
                need(v, tr_done, st.m - 3)
                need(v, carry_steps, st.m * K_CARRY)
                c = ck.at(st.m * K_CARRY)
                carry_rows(v, c, lambda t: XD[:, s, t], DR[:, s], KF[:, s],
                           [(t, XD[:, s, t + 1] if t < B - 1 else XD[:, prev, 0]) for t in order])
                assert c.n == K_CARRY

            def args(st):
                s, prev = st.slot, (st.slot - 1) % SLOTS
                v.wait_ge(lg_done, st.m + 1)
                v.wait_ge(flags_in, st.m + 1)
                need(v, args_steps, st.m * K_ARGS)
                need(v, exp_done, st.m - 3)
                c = ca.at(st.m * K_ARGS)
                lg = pL[0:EP, 0:2 * H * B].rearrange("p (t i h) -> p t i h", t=B, i=2)
                c.put(v.tensor_copy(MH[:, s, begin], MH[:, prev, end]))
                c.put(v.tensor_tensor(EM[:, s], lg[:, :, 1], FB[:, s, :, 1].unsqueeze(2).to_broadcast([EP, B, H]), ALU.add))
                c.sync()
                c.put(v.tensor_tensor(D1[:, s], lg[:, :, 0], EM[:, s], ALU.max))
                c.sync()
                for t in order:
                    c.put(v.scalar_tensor_tensor(MH[:, s, t + own], MH[:, s, t + old], FB[:, s, t, 0:1], D1[:, s, t], ALU.add, ALU.max))
                    c.sync()
                c.put(v.tensor_tensor(CB[:, s], MH[:, s, old:old + B], FB[:, s, :, 0].unsqueeze(2).to_broadcast([EP, B, H]), ALU.add))
                c.put(v.tensor_tensor(A[:, s, :, 0:H], lg[:, :, 0], MH[:, s, own:own + B], ALU.subtract))
                c.put(v.tensor_tensor(A[:, s, :, H:2 * H], EM[:, s], MH[:, s, own:own + B], ALU.subtract))
                c.sync()
                c.put(v.tensor_tensor(A[:, s, :, 2 * H:3 * H], CB[:, s], MH[:, s, own:own + B], ALU.subtract))
                assert c.n == K_ARGS, c.n

            def leaky(st):
                p = st.slot % 2
                v.wait_ge(fifth_ready, st.m + 1)
                for i, of in enumerate((pS, pD)):
                    last = v.tensor_tensor(lr[:, p, i], of[:, 0:B * EP], lr[:, p, i], ALU.max)
                last.then_inc(lr_ready, 1)

            def main(st):
                s, prev, p = st.slot, (st.slot - 1) % SLOTS, st.slot % 2
                v.wait_ge(exp_done, st.m + 1)
                v.wait_ge(v_done, st.m + 1)
                need(v, piece_ready, st.m - 3)
                need(v, main_steps, st.m * K_MAIN)
                c = cm.at(st.m * K_MAIN)
                w = heads(Wt[:, p])
                ex, sf = XE[:, s, :, 0:H], XE[:, s, :, H:2 * H]
                c.put(v.tensor_tensor(w[:, :, :, 0:C], heads(pV[0:EP, :].rearrange("p (t f) -> p t f", t=B)), over(ex, C), ALU.mult))
                c.put(v.tensor_tensor(heads(W2[:, p]), heads(pU[0:EP, :].rearrange("p (t f) -> p t f", t=B)), over(sf, C), ALU.mult))
                c.put(v.tensor_tensor(w[:, :, :, C], ex, sf, ALU.add))
                c.sync()
                c.put(v.tensor_tensor(w[:, :, :, 0:C], w[:, :, :, 0:C], heads(W2[:, p]), ALU.add))
                for i, t in enumerate(order):
                    before = ST[:, s, order[i - 1], 0:HW] if i else ST[:, prev, order[-1], 0:HW]
                    c.put(v.tensor_tensor(prod[:, :].rearrange("p (h c) -> p h c", h=H), before.rearrange("p (h c) -> p h c", h=H),
                                          XE[:, s, t, 2 * H:3 * H].unsqueeze(2).to_broadcast([EP, H, C + 1]), ALU.mult))
                    c.sync()
                    c.put(v.tensor_tensor(ST[:, s, t, 0:HW], prod[:, :], Wt[:, p, t], ALU.add))
                    c.sync()
                need(v, rows_out[s], 16 * B * st.k)
                need(v, dr_out[s], 16 * st.k)
                finish(v, c, heads(ST[:, s, :, 0:HW]), B, O[:, s], den[:, p], None, split=back)
                assert c.n == K_MAIN, c.n

            def add_x(st):
                v.wait_ge(bias_in, st.m + 1)
                v.wait_ge(xe[st.slot], 16 * (st.k + 1))
                v.scalar_tensor_tensor(O[:, st.slot], O[:, st.slot], 0.0, XR[:, st.slot], ALU.max, ALU.add).then_inc(x_added, 1)

            run_steps(v, NB, [(3, main), (0, carry), (1, leaky), (2, args), (4, add_x)] if back else [(3, main), (1, leaky), (2, args)])
            v.wait_ge(piece_done, NB)
            v.tensor_copy(F[:, :], pF[0:EP, 0:HS]).then_inc(piece_in, 1)
            v.wait_ge(piece_in, 1)
            if res_t is not None:
                v.wait_ge(join_in, 32)
            join_vec(v, OJ[:, :, :])

        blocks.close()
        clear_semaphores(nc, used)


def edge_attention(nc, k):
    H, C = 1, P
    HW, HS = C + 1, C + 2
    T, NB, N = k.T, k.NB, k.N
    DEEP = 2 * SLOTS
    R = 2 * B
    K_TAKE = R + 7
    K_CENTRE = R + 8
    K_SCALE = 4
    K_ARGS = 3 + B + 1
    K_MAIN = 2 * B + 4
    W = k.W
    used = []
    with ExitStack() as ctx, ExitStack() as blocks:
        def sb(name, shape, dt=F32):
            return ctx.enter_context(nc.sbuf_tensor("e_" + name, list(shape), dt))

        def sem(name):
            if name.rstrip("0123") in k.by_pool_dma:
                return k.whole.enter_context(nc.semaphore(name + "_e"))
            used.append(ctx.enter_context(nc.semaphore(name + "_e")))
            return used[-1]

        IB = sb("IB", [EP, SLOTS, B], I32)
        OB = sb("OB", [EP, SLOTS, B], I32)
        FB = sb("FB", [EP, SLOTS, B, 3])
        KF = sb("KF", [EP, SLOTS, B, 2])
        DR = sb("DR", [EP, SLOTS, B, P])
        back_row = sb("back_row", [EP, P])
        XX = sb("XX", [EP, DEEP, R, P])
        bn = sb("bn", [EP, R, 6])
        tmpm = sb("tmpm", [EP, 3, R])
        bnu, tmpu = sb("bnu", [EP, R, 6]), sb("tmpu", [EP, 3, R])
        vpe, mu, vu, r1, rr = (sb(n, [EP, DEEP, R]) for n in ("vpe", "mu", "vu", "r1", "rr"))
        eps2 = sb("eps2", [EP, R])
        nmean, nmr = sb("nmean", [EP, DEEP, R]), sb("nmr", [EP, DEEP, R])
        g4 = sb("g4", [EP, DEEP, R, 4])
        ex6 = sb("ex6", [EP, DEEP, B, 6])
        dg = sb("deg_ends", [EP, 2])
        GE = sb("GE", [EP, SLOTS, B, P])
        hT = sb("hT", [P, SLOTS, 2, B * EP])
        exT = sb("exT", [6, SLOTS, B * EP])
        xiT = sb("xiT", [P, 2, B * EP])
        MH = sb("MH", [EP, SLOTS, B + 1])
        CB = sb("CB", [EP, SLOTS, B])
        A, XE = sb("A", [EP, SLOTS, 2, B]), sb("XE", [EP, SLOTS, 2, B])
        Wt = sb("Wt", [EP, 2, B, HW])
        ST = sb("ST", [EP, SLOTS, B, HS])
        F = sb("F", [EP, HS])
        den = sb("den", [EP, 2, B])
        O = sb("O", [EP, SLOTS, B, P])
        OJ, GJ = sb("OJ", [EP, 2, P]), sb("GJ", [EP, 2, P])
        pS, pD, pX, pG, pQ, pL = (ctx.enter_context(nc.psum_tensor("e_" + n, [P, 512], F32)) for n in ("pS", "pD", "pX", "pG", "pQ", "pL"))
        pV = [ctx.enter_context(nc.psum_tensor(f"e_pV{i}", [P, 512], F32)) for i in range(2)]
        gat = [sem(f"gat{s}") for s in range(SLOTS)]
        dr_in = [sem(f"dr_in{s}") for s in range(SLOTS)]
        keep_in, carry_steps, masked, weighed = (sem(n) for n in ("keep_in", "carry_steps", "masked", "weighed"))
        K_CARRY = 1 + B
        rows_from = k.dst_rows[1].rearrange("(p t) f -> p t f", t=T)
        rows_out = [sem(f"rows_out{s}") for s in range(SLOTS)]
        (idx_in, flags_in, r1_in, r2_in, tr_done, hT_ready, mm_done, xi_ready, v_done, exp_done,
         take_steps, centre_steps, scale_steps, args_steps, main_steps, init, join_out, gj_arg, gj_exp, passed, u_ready, h_ready, gate_done, gate_ready) = (
            sem(n) for n in ("idx_in", "flags_in", "r1_in", "r2_in", "tr_done", "hT_ready", "mm_done", "xi_ready", "v_done",
                             "exp_done", "take_steps", "centre_steps", "scale_steps", "args_steps", "main_steps", "init", "join_out",
                             "gj_arg", "gj_exp", "passed", "u_ready", "h_ready", "gate_done", "gate_ready"))
        k.join_ps = (pS, pD)

        def finish(v, c, acc, n, out, dn, ge):
            c.put(v.tensor_scalar(dn, acc[:, :, C], 1e-9, 2.0, ALU.add, ALU.mult))
            c.sync()
            c.put(v.reciprocal(dn, dn))
            c.sync()
            c.put(v.tensor_tensor(out, acc[:, :, 0:C], dn.unsqueeze(2).to_broadcast([EP, n, C]), ALU.mult))
            c.sync()
            c.put(v.scalar_tensor_tensor(out, ge, 3.0, out, ALU.add, ALU.mult))

        def join_finish(v, c, acc, n, out):
            for i in range(2):
                c.put(v.scalar_tensor_tensor(GJ[:, i], k.row["w_g"][0:EP, :], dg[:, i:i + 1], k.row["b_g"][0:EP, :], ALU.mult, ALU.add))
            c.sync()
            v.sem_inc(gj_arg, 1)
            v.wait_ge(gj_exp, 1)
            finish(v, c, acc.rearrange("p n h c -> p n (h c)"), n, out, den[:, 0, 0:2], GJ[:, :, :])

        join_vec, join_pe, join_act, join_pool = join_pieces(
            nc, k, "e_", H, C, ST[:, (NB - 1) % SLOTS, B - 1], F, ctx, sem, (main_steps, NB * K_MAIN), join_finish)
        block = blocks.enter_context(nc.Block())

        @block.sync
        def _(sp):
            def load_rows(st):
                need(sp, carry_steps, (st.m - 3) * K_CARRY)
                sp.dma_start(DR[:, st.slot], rows_from[:, bass.ds(st.m * B, B), :]).then_inc(dr_in[st.slot], 16)

            run_steps(sp, NB, [(0, load_rows)], DEEP)

        @block.gpsimd
        def _(pool):
            last_row = pool.to_reg(N - 1)

            def fetch(st):
                s = st.slot
                need(pool, gat[s], 16 * B * st.k)
                pool.tensor_copy(IB[:, s], k.idx[:, bass.ds(st.m * B, B), 0]).then_inc(idx_in, 1)
                need(pool, carry_steps, (st.m - 3) * K_CARRY)
                pool.tensor_copy(KF[:, s], k.flag[:, bass.ds(st.m * B, B), 0:2]).then_inc(keep_in, 1)
                pool.wait_ge(idx_in, st.m + 1)
                need(pool, tr_done, st.m - 7)
                stand_alone(pool, passed)
                for t in range(B):
                    gather(pool, XX[:, st.wslot, t], k.x1_t, IB[:, s, t:t + 1], last_row).then_inc(gat[s], 16)

            def rsqrt1(st):
                pool.wait_ge(take_steps, (st.m + 1) * K_TAKE)
                pool.tensor_tensor(r1[:, st.wslot], vpe[:, st.wslot], k.half[0:EP, 0:R], ALU.pow).then_inc(r1_in, 1)

            def rsqrt2(st):
                pool.wait_ge(centre_steps, (st.m + 1) * K_CENTRE)
                pool.tensor_tensor(rr[:, st.wslot], vu[:, st.wslot], k.half[0:EP, 0:R], ALU.pow).then_inc(r2_in, 1)

            def flags(st):
                s = st.slot
                need(pool, rows_out[s], 16 * B * st.k)
                pool.tensor_copy(OB[:, s], k.idx[:, bass.ds(st.m * B, B), 4])
                need(pool, main_steps, (st.m - 3) * K_MAIN)
                pool.tensor_copy(FB[:, s], k.flag[:, bass.ds(st.m * B, B), 2:5]).then_inc(flags_in, 1)

            def write_rows(st):
                pool.wait_ge(flags_in, st.m + 1)
                pool.wait_ge(main_steps, (st.m + 1) * K_MAIN)
                stand_alone(pool, passed)
                for t in range(B):
                    pool.indirect_dma_start(k.z_t[0:N, :], bass.IndirectOffsetOnAxis(OB[:, st.slot, t:t + 1], 0), O[:, st.slot, t], None,
                                            bounds_check=last_row, oob_is_err=False).then_inc(rows_out[st.slot], 16)

            run_steps(pool, NB, [(0, fetch), (7, flags), (3, rsqrt2), (1, rsqrt1), (10, write_rows)], DEEP)
            join_pool(pool, OJ, k.z_t[0:N, :], join_out, last_row)
            for s in range(SLOTS):
                pool.wait_ge(rows_out[s], 16 * B * ((NB - 1 - s) // SLOTS + 1))

        @block.tensor
        def _(pe):
            def turn(st):
                s = st.slot
                pe.wait_ge(h_ready, st.m + 1)
                need(pe, hT_ready, st.m)
                for i, to in enumerate((pS, pD)):
                    for t in range(B):
                        nc.tensor.transpose(to[:, t * EP:(t + 1) * EP], XX[:, st.wslot, i * B + t], k.ident[0:EP, 0:EP])
                for t in range(B):
                    last = nc.tensor.transpose(pX[0:6, t * EP:(t + 1) * EP], ex6[:, st.wslot, t], k.ident[0:EP, 0:EP])
                last.then_inc(tr_done, 1)

            def project(st):
                s = st.slot
                pe.wait_ge(hT_ready, st.m + 1)
                need(pe, xi_ready, st.m)
                nc.tensor.matmul(pQ[:, 0:B * EP], W["WQT"][:, :], hT[:, s, 1], start=True, stop=False)
                nc.tensor.matmul(pQ[:, 0:B * EP], W["WKT"][:, :], hT[:, s, 0], start=False, stop=False)
                nc.tensor.matmul(pQ[:, 0:B * EP], k.WS6[:, :], exT[:, s], start=False, stop=True).then_inc(mm_done, 1)
                need(pe, gate_ready, st.m)
                for t in range(B):
                    last = nc.tensor.matmul(pG[0:EP, t * P:(t + 1) * P], exT[:, s, t * EP:(t + 1) * EP], k.WG6[:, :], start=True, stop=True)
                last.then_inc(gate_done, 1)

            def values(st):
                p = st.slot % 2
                pe.wait_ge(xi_ready, st.m + 1)
                need(pe, weighed, st.m - 1)
                need(pe, args_steps, st.m * K_ARGS)
                for t in range(B):
                    xi = xiT[:, p, t * EP:(t + 1) * EP]
                    nc.tensor.matmul(pV[p][0:EP, t * P:(t + 1) * P], hT[:, st.slot, 0, t * EP:(t + 1) * EP], W["WVT"][:, :], start=True, stop=False)
                    nc.tensor.matmul(pV[p][0:EP, t * P:(t + 1) * P], xi, W["WET"][:, :], start=False, stop=True)
                    last = nc.tensor.matmul(pL[0:EP, t:t + 1], xi, k.col["w_a"][:, :], start=True, stop=True)
                last.then_inc(v_done, 1)

            run_steps(pe, NB, [(8, values), (6, turn), (7, project)], DEEP)
            join_pe(pe)

        @block.scalar
        def _(act):
            def affine_rows(st):
                s = st.slot
                act.wait_ge(tr_done, st.m + 1)
                need(act, v_done, st.m - 3)
                for i, of in enumerate((pS, pD)):
                    act.activation(hT[:, s, i], of[:, 0:B * EP], ACT.Identity, bias=k.col["ln1_b"][:, :], scale=k.col["ln1_g"][:, :])
                act.activation(exT[:, s], pX[0:6, 0:B * EP], ACT.Copy).then_inc(hT_ready, 1)

            def relu_xi(st):
                act.wait_ge(mm_done, st.m + 1)
                need(act, v_done, st.m - 1)
                act.activation(xiT[:, st.slot % 2], pQ[:, 0:B * EP], ACT.Relu).then_inc(xi_ready, 1)

            def exps(st):
                s = st.slot
                act.wait_ge(args_steps, (st.m + 1) * K_ARGS)
                need(act, main_steps, (st.m - 3) * K_MAIN)
                act.activation(XE[:, s], A[:, s], ACT.Exp).then_inc(exp_done, 1)

            def gate(st):
                act.wait_ge(gate_done, st.m + 1)
                need(act, main_steps, (st.m - 3) * K_MAIN)
                act.activation(GE[:, st.slot], pG[0:EP, :].rearrange("p (t f) -> p t f", t=B), ACT.Tanh, scale=0.5).then_inc(gate_ready, 1)

            def centre_rows(st):
                act.wait_ge(take_steps, (st.m + 1) * K_TAKE)
                for i in range(R):
                    last = act.activation(XX[:, st.wslot, i], XX[:, st.wslot, i], ACT.Relu, bias=nmean[:, st.wslot, i:i + 1])
                last.then_inc(u_ready, 1)

            def scale_rows(st):
                act.wait_ge(scale_steps, (st.m + 1) * K_SCALE)
                for i in range(R):
                    last = act.activation(XX[:, st.wslot, i], XX[:, st.wslot, i], ACT.Identity, bias=nmr[:, st.wslot, i:i + 1],
                                          scale=rr[:, st.wslot, i:i + 1])
                last.then_inc(h_ready, 1)

            def mask(st):
                act.wait_ge(dr_in[st.slot], 16 * (st.k + 1))
                act.wait_ge(keep_in, st.m + 1)
                mask_rows(act, DR[:, st.slot], KF[:, st.slot]).then_inc(masked, 1)

            def weigh(st):
                s, p = st.slot, st.slot % 2
                act.wait_ge(exp_done, st.m + 1)
                act.wait_ge(v_done, st.m + 1)
                need(act, main_steps, (st.m - 1) * K_MAIN)
                act.activation(ST[:, s, :, HW], MH[:, s, 1:B + 1], ACT.Copy)
                act.activation(Wt[:, p, :, C], XE[:, s, 0], ACT.Copy)
                for t in range(B):
                    last = act.activation(Wt[:, p, t, 0:C], pV[p][0:EP, t * P:(t + 1) * P], ACT.Copy, scale=XE[:, s, 0, t:t + 1])
                last.then_inc(weighed, 1)

            run_steps(act, NB, [(0, mask), (5, scale_rows), (2, centre_rows), (6, affine_rows), (7, relu_xi), (7, gate), (8, exps), (8, weigh)], DEEP)
            join_act(act)
            act.wait_ge(gj_arg, 1)
            act.activation(GJ[:, :, :], GJ[:, :, :], ACT.Tanh, scale=0.5).then_inc(gj_exp, 1)

        @block.vector
        def _(v):
            v.memset(MH[:, SLOTS - 1], 0.0).then_inc(init, 1)
            v.memset(ST[:, SLOTS - 1], 0.0).then_inc(init, 1)
            v.memset(F[:, :], 0.0).then_inc(init, 1)
            v.memset(ex6[:, :, :, :], 1.0).then_inc(init, 1)
            v.memset(back_row[:, :], 0.0).then_inc(init, 1)
            v.wait_ge(init, 5)
            ck = Chain(v, carry_steps)
            ct, cc, cs, ca, cm = (Chain(v, x) for x in (take_steps, centre_steps, scale_steps, args_steps, main_steps))

            def carry(st):
                s = st.slot
                v.wait_ge(masked, st.m + 1)
                need(v, tr_done, st.m - 7)
                need(v, carry_steps, st.m * K_CARRY)
                c = ck.at(st.m * K_CARRY)
                carry_rows(v, c, lambda t: XX[:, st.wslot, B + t], DR[:, s], KF[:, s],
                           [(t, XX[:, st.wslot, B + t - 1] if t else back_row[:, :]) for t in range(B)])
                c.put(v.tensor_copy(back_row[:, :], XX[:, st.wslot, R - 1]))
                assert c.n == K_CARRY

            def take(st):
                s = st.slot
                v.wait_ge(gat[s], 16 * B * (st.k + 1))
                v.wait_ge(carry_steps, (st.m + 1) * K_CARRY)
                c = ct.at(st.m * K_TAKE)
                need(v, take_steps, st.m * K_TAKE)
                for i in range(R):
                    c.put(v.bn_stats(bn[:, i], XX[:, st.wslot, i]))
                c.sync()
                moments(v, c, bn, nmean[:, st.wslot], vpe[:, st.wslot], tmpm, sign=-1.0)
                assert c.n == K_TAKE

            def centre(st):
                s = st.slot
                v.wait_ge(u_ready, st.m + 1)
                need(v, centre_steps, st.m * K_CENTRE)
                c = cc.at(st.m * K_CENTRE)
                c.put(v.tensor_scalar(eps2[:, :], vpe[:, st.wslot], EPS, None, ALU.mult))
                for i in range(R):
                    c.put(v.bn_stats(bnu[:, i], XX[:, st.wslot, i]))
                c.sync()
                moments(v, c, bnu, mu[:, st.wslot], vu[:, st.wslot], tmpu, eps=eps2[:, :])
                assert c.n == K_CENTRE

            def scale(st):
                s = st.slot
                v.wait_ge(r1_in, st.m + 1)
                v.wait_ge(r2_in, st.m + 1)
                need(v, tr_done, st.m - 7)
                c = cs.at(st.m * K_SCALE)
                c.put(v.tensor_tensor(g4[:, st.wslot], XX[:, st.wslot, :, P - 4:P], r1[:, st.wslot].unsqueeze(2).to_broadcast([EP, R, 4]), ALU.mult))
                c.sync()
                c.put(v.scalar_tensor_tensor(nmr[:, st.wslot], mu[:, st.wslot], -1.0, rr[:, st.wslot], ALU.mult, ALU.mult))
                c.put(v.tensor_tensor(ex6[:, st.wslot, :, 2:6], g4[:, st.wslot, B:R], g4[:, st.wslot, 0:B], ALU.subtract))
                c.put(v.tensor_copy(ex6[:, st.wslot, :, 0], g4[:, st.wslot, B:R, 0]))
                if st.first:
                    v.tensor_copy(dg[:, 1:2], g4[:, st.wslot, B, 0:1])
                if st.last:
                    v.tensor_copy(dg[:, 0:1], g4[:, st.wslot, R - 1, 0:1])
                assert c.n == K_SCALE, c.n

            def args(st):
                s, prev = st.slot, (st.slot - 1) % SLOTS
                v.wait_ge(v_done, st.m + 1)
                v.wait_ge(flags_in, st.m + 1)
                need(v, args_steps, st.m * K_ARGS)
                need(v, exp_done, st.m - 3)
                c = ca.at(st.m * K_ARGS)
                lg = pL[0:EP, 0:B]
                c.put(v.tensor_copy(MH[:, s, 0:1], MH[:, prev, B:B + 1]))
                c.sync()
                for t in range(B):
                    c.put(v.scalar_tensor_tensor(MH[:, s, t + 1:t + 2], MH[:, s, t:t + 1], FB[:, s, t, 0:1], pL[0:EP, t:t + 1], ALU.add, ALU.max))
                    c.sync()
                c.put(v.tensor_tensor(CB[:, s], MH[:, s, 0:B], FB[:, s, :, 0], ALU.add))
                c.put(v.tensor_tensor(A[:, s, 0], lg, MH[:, s, 1:B + 1], ALU.subtract))
                c.sync()
                c.put(v.tensor_tensor(A[:, s, 1], CB[:, s], MH[:, s, 1:B + 1], ALU.subtract))
                assert c.n == K_ARGS, c.n

            def main(st):
                s, prev, p = st.slot, (st.slot - 1) % SLOTS, st.slot % 2
                v.wait_ge(weighed, st.m + 1)
                v.wait_ge(gate_ready, st.m + 1)
                need(v, main_steps, st.m * K_MAIN)
                c = cm.at(st.m * K_MAIN)
                for t in range(B):
                    before = ST[:, s, t - 1, 0:HW] if t else ST[:, prev, B - 1, 0:HW]
                    c.put(v.scalar_tensor_tensor(ST[:, s, t, 0:HW], before, XE[:, s, 1, t:t + 1], Wt[:, p, t], ALU.mult, ALU.add))
                    c.sync()
                    c.put(v.scalar_tensor_tensor(F[:, :], ST[:, s, t], FB[:, s, t, 2:3], F[:, :], ALU.mult, ALU.add))
                need(v, rows_out[s], 16 * B * st.k)
                finish(v, c, ST[:, s, :, 0:HW], B, O[:, s], den[:, p], GE[:, s])
                assert c.n == K_MAIN, c.n

            run_steps(v, NB, [(4, scale), (1, take), (3, centre), (0, carry), (8, args), (9, main)], DEEP)
            join_vec(v, OJ[:, :, :])

        blocks.close()
        clear_semaphores(nc, used)


def ffn_pass(nc, k):
    N, NG = k.N, k.NG
    K_TAKE = J + 7
    K_CENTRE = 3 * J + 7
    K_SCALE = J
    used = []
    with ExitStack() as ctx, ExitStack() as blocks:
        def sb(name, shape, dt=F32):
            return ctx.enter_context(nc.sbuf_tensor("f_" + name, list(shape), dt))

        def sem(name):
            used.append(ctx.enter_context(nc.semaphore(name + "_f")))
            return used[-1]

        X = sb("X", [P, SLOTS, J, P])
        Z, Y, O = (sb(n, [P, SLOTS, J, P]) for n in ("Z", "Y", "O"))
        bn = sb("bn", [P, 2, J, 6])
        tmpm = sb("tmpm", [P, 3, J])
        mean, vpe, mu, vu, r1, r2 = (sb(n, [P, SLOTS, J]) for n in ("mean", "vpe", "mu", "vu", "r1", "r2"))
        HN = sb("HN", [P, 2, J, P])
        total, tail = sb("total", [P, J, P]), sb("tail", [P, J, P])
        hT, fT = sb("hT", [P, 2, GROUP]), sb("fT", [P, 2, GROUP])
        GT = sb("GT", [P, 2, 4, GROUP])
        pT, pF, pN, pG = (ctx.enter_context(nc.psum_tensor("f_" + n, [P, 512], F32)) for n in ("pT", "pF", "pN", "pG"))
        pH = [ctx.enter_context(nc.psum_tensor(f"f_pH{i}", [P, 512], F32)) for i in range(4)]
        rows_in = [sem(f"rows_in{s}") for s in range(SLOTS)]
        y2_out = [sem(f"y2_out{s}") for s in range(SLOTS)]
        (r1_in, r2_in, take_steps, centre_steps, scale_steps, y2_ready, tr_done, hT_ready, up_done, gelu_ready, down_done,
         fT_ready, back_done, sum_done, gsum_in, total_init, total_summed, tail_in) = (
            sem(n) for n in ("r1_in", "r2_in", "take_steps", "centre_steps", "scale_steps", "y2_ready", "tr_done", "hT_ready",
                             "up_done", "gelu_ready", "down_done", "fT_ready", "back_done", "sum_done", "gsum_in", "total_init", "total_summed", "tail_in"))
        block = blocks.enter_context(nc.Block())

        @block.sync
        def _(sp):
            def load(st):
                need(sp, centre_steps, (st.m - 3) * K_CENTRE)
                sp.dma_start(X[:, st.slot], k.rows_of(k.x1_t, st)).then_inc(rows_in[st.slot], 16)
                sp.dma_start(Z[:, st.slot], k.rows_of(k.z_t[0:N, :], st)).then_inc(rows_in[st.slot], 16)

            def store(st):
                sp.wait_ge(y2_ready, st.m + 1)
                if st.last:
                    sp.wait_ge(y2_out[(st.m - 1) % SLOTS], 16 * ((st.m - 1) // SLOTS + 1))
                sp.dma_start(k.rows_of(k.y2_t, st), O[:, st.slot]).then_inc(y2_out[st.slot], 16)

            run_steps(sp, NG, [(0, load), (6, store)])
            for s in range(SLOTS):
                sp.wait_ge(y2_out[s], 16 * ((NG - 1 - s) // SLOTS + 1))

        @block.gpsimd
        def _(pool):
            def rsqrt1(st):
                pool.wait_ge(take_steps, (st.m + 1) * K_TAKE)
                pool.tensor_tensor(r1[:, st.slot], vpe[:, st.slot], k.half[:, 0:J], ALU.pow).then_inc(r1_in, 1)

            def rsqrt2(st):
                pool.wait_ge(centre_steps, (st.m + 1) * K_CENTRE)
                pool.tensor_tensor(r2[:, st.slot], vu[:, st.slot], k.half[:, 0:J], ALU.pow).then_inc(r2_in, 1)

            def add_rows(st):
                pool.wait_ge(y2_ready, st.m + 1)
                need(pool, sum_done, st.m)
                rows = O[:, st.slot]
                if st.last:
                    pool.tensor_scalar(tail[:, :, :], rows, k.tail_ones[:, 0:1], None, ALU.mult).then_inc(tail_in, 1)
                    pool.wait_ge(tail_in, 1)
                    rows = tail[:, :, :]
                pool.tensor_tensor(total[:, :, :], total[:, :, :], rows, ALU.add).then_inc(sum_done, 1)

            pool.memset(total[:, :, :], 0.0).then_inc(total_init, 1)
            pool.wait_ge(total_init, 1)
            run_steps(pool, NG, [(1, rsqrt2), (0, rsqrt1), (6, add_rows)])

        @block.vector
        def _(v):
            ct, cc, cs = (Chain(v, x) for x in (take_steps, centre_steps, scale_steps))

            def take(st):
                s, p = st.slot, st.slot % 2
                v.wait_ge(rows_in[s], 32 * (st.k + 1))
                need(v, centre_steps, (st.m - 1) * K_CENTRE)
                c = ct.at(st.m * K_TAKE)
                for j in range(J):
                    c.put(v.bn_stats(bn[:, p, j], X[:, s, j]))
                c.sync()
                moments(v, c, bn[:, p], mean[:, s], vpe[:, s], tmpm)

            def centre(st):
                s, p = st.slot, st.slot % 2
                v.wait_ge(r1_in, st.m + 1)
                c = cc.at(st.m * K_CENTRE)
                for j in range(J):
                    c.put(v.tensor_scalar(X[:, s, j], X[:, s, j], mean[:, s, j:j + 1], 0.0, ALU.subtract, ALU.max))
                c.sync()
                need(v, y2_ready, st.m - 3)
                for j in range(J):
                    c.put(v.scalar_tensor_tensor(Y[:, s, j], X[:, s, j], r1[:, s, j:j + 1], Z[:, s, j], ALU.mult, ALU.add))
                c.sync()
                for j in range(J):
                    c.put(v.bn_stats(bn[:, p, j], Y[:, s, j]))
                c.sync()
                moments(v, c, bn[:, p], mu[:, s], vu[:, s], tmpm)

            def scale(st):
                s, p = st.slot, st.slot % 2
                v.wait_ge(r2_in, st.m + 1)
                need(v, tr_done, st.m - 1)
                c = cs.at(st.m * K_SCALE)
                for j in range(J):
                    c.put(v.tensor_scalar(HN[:, p, j], Y[:, s, j], mu[:, s, j:j + 1], r2[:, s, j:j + 1], ALU.subtract, ALU.mult))

            def add_ffn(st):
                v.wait_ge(back_done, st.m + 1)
                need(v, y2_out[st.slot], 16 * st.k)
                need(v, sum_done, st.m - 3)
                v.tensor_tensor(O[:, st.slot], Y[:, st.slot], pN[:, :].rearrange("p (j f) -> p j f", j=J), ALU.add).then_inc(y2_ready, 1)

            run_steps(v, NG, [(2, scale), (5, add_ffn), (1, centre), (0, take)])
            v.wait_ge(total_summed, 1)
            v.tensor_scalar(k.gsum[:, :], pG[:, 0:1], 1.0 / N, None, ALU.mult).then_inc(gsum_in, 1)
            v.wait_ge(gsum_in, 1)

        @block.tensor
        def _(pe):
            def turn(st):
                p = st.slot % 2
                pe.wait_ge(scale_steps, (st.m + 1) * K_SCALE)
                need(pe, hT_ready, st.m)
                for j in range(J):
                    last = nc.tensor.transpose(pT[:, j * P:(j + 1) * P], HN[:, p, j], k.ident[:, :])
                last.then_inc(tr_done, 1)

            def up(st):
                pe.wait_ge(hT_ready, st.m + 1)
                for c in range(4):
                    need(pe, gelu_ready, (st.m - 1) * 4 + c + 1)
                    nc.tensor.matmul(pH[c][:, :], k.F1T[:, c], hT[:, st.slot % 2], start=True, stop=True).then_inc(up_done, 1)

            def down(st):
                need(pe, fT_ready, st.m)
                for c in range(4):
                    pe.wait_ge(gelu_ready, st.m * 4 + c + 1)
                    last = nc.tensor.matmul(pF[:, :], k.F2T[:, c], GT[:, st.slot % 2, c], start=c == 0, stop=c == 3)
                last.then_inc(down_done, 1)

            def turn_back(st):
                pe.wait_ge(fT_ready, st.m + 1)
                need(pe, y2_ready, st.m)
                for j in range(J):
                    last = nc.tensor.transpose(pN[:, j * P:(j + 1) * P], fT[:, st.slot % 2, j * P:(j + 1) * P], k.ident[:, :])
                last.then_inc(back_done, 1)

            run_steps(pe, NG, [(4, down), (2, turn), (3, up), (4, turn_back)])
            pe.wait_ge(sum_done, NG)
            for j in range(J):
                last = nc.tensor.matmul(pG[:, 0:1], total[:, j], k.ones[:, 0:1], start=j == 0, stop=j == J - 1)
            last.then_inc(total_summed, 1)

        @block.scalar
        def _(act):
            def affine(st):
                act.wait_ge(tr_done, st.m + 1)
                need(act, up_done, (st.m - 1) * 4)
                act.activation(hT[:, st.slot % 2], pT[:, :], ACT.Identity, bias=k.col["ln2_b"][:, :], scale=k.col["ln2_g"][:, :]).then_inc(hT_ready, 1)

            def gelu(st):
                need(act, down_done, st.m - 1)
                for c in range(4):
                    act.wait_ge(up_done, st.m * 4 + c + 1)
                    act.activation(GT[:, st.slot % 2, c], pH[c][:, :], ACT.Gelu, bias=k.fb1[:, c:c + 1]).then_inc(gelu_ready, 1)

            def down_bias(st):
                act.wait_ge(down_done, st.m + 1)
                need(act, back_done, st.m - 1)
                act.activation(fT[:, st.slot % 2], pF[:, :], ACT.Identity, bias=k.col["ffn_b2"][:, :]).then_inc(fT_ready, 1)

            run_steps(act, NG, [(4, down_bias), (2, affine), (3, gelu)])

        blocks.close()
        clear_semaphores(nc, used)


def squeeze_and_out(nc, k):
    NG = k.NG
    used = []
    with ExitStack() as ctx, ExitStack() as blocks:
        def sb(name, shape, dt=F32):
            return ctx.enter_context(nc.sbuf_tensor("o_" + name, list(shape), dt))

        def sem(name):
            used.append(ctx.enter_context(nc.semaphore(name + "_o")))
            return used[-1]

        X, Y, O = (sb(n, [P, SLOTS, J, P]) for n in ("X", "Y", "O"))
        s1, s2, s3, nb2 = sb("s1", [32, 1]), sb("s2", [P, 1]), sb("s3", [P, 1]), sb("nb2", [P, 1])
        dg = sb("dg", [P, P])
        ps = ctx.enter_context(nc.psum_tensor("o_ps", [P, 512], F32))
        pr = ctx.enter_context(nc.psum_tensor("o_pr", [P, 512], F32))
        rows_in = [sem(f"rows_in{s}") for s in range(SLOTS)]
        rows_out = [sem(f"rows_out{s}") for s in range(SLOTS)]
        squeeze_pe, squeeze_act, squeeze_vec, mults, sums = (sem(n) for n in ("squeeze_pe", "squeeze_act", "squeeze_vec", "mults", "sums"))
        block = blocks.enter_context(nc.Block())

        @block.sync
        def _(sp):
            def load(st):
                need(sp, sums, st.m - 3)
                sp.dma_start(X[:, st.slot], k.rows_of(k.x1_t, st)).then_inc(rows_in[st.slot], 16)
                sp.dma_start(Y[:, st.slot], k.rows_of(k.y2_t, st)).then_inc(rows_in[st.slot], 16)

            run_steps(sp, NG, [(0, load)])

        @block.tensor
        def _(pe):
            nc.tensor.matmul(ps[0:32, 0:1], k.S1T[:, :], k.gsum[:, :], start=True, stop=True).then_inc(squeeze_pe, 1)
            pe.wait_ge(squeeze_act, 1)
            nc.tensor.matmul(ps[:, 1:2], k.S2T[:, :], s1[:, :], start=True, stop=True).then_inc(squeeze_pe, 1)
            pe.wait_ge(squeeze_vec, 4)
            nc.tensor.matmul(pr[:, 0:P], k.ones[:, :], dg[:, :], start=True, stop=True).then_inc(squeeze_pe, 1)

        @block.scalar
        def _(act):
            act.wait_ge(squeeze_pe, 1)
            act.activation(s1[:, :], ps[0:32, 0:1], ACT.Relu, bias=k.seb1[:, :]).then_inc(squeeze_act, 1)
            act.wait_ge(squeeze_pe, 2)
            act.wait_ge(squeeze_vec, 1)
            act.activation(s2[:, :], ps[:, 1:2], ACT.Exp, scale=-1.0, bias=nb2[:, :]).then_inc(squeeze_act, 1)

            def store(st):
                act.wait_ge(sums, st.m + 1)
                if st.last:
                    act.wait_ge(rows_out[(st.m - 1) % SLOTS], 16 * ((st.m - 1) // SLOTS + 1))
                act.dma_start(k.rows_of(k.a["out"], st), O[:, st.slot]).then_inc(rows_out[st.slot], 16)

            run_steps(act, NG, [(0, store)])
            for s in range(SLOTS):
                act.wait_ge(rows_out[s], 16 * ((NG - 1 - s) // SLOTS + 1))

        @block.vector
        def _(v):
            c = Chain(v, squeeze_vec)
            c.put(v.tensor_scalar(nb2[:, :], k.col["se_b2"][:, :], -1.0, None, ALU.mult))
            v.wait_ge(squeeze_act, 2)
            c.put(v.tensor_scalar(s3[:, :], s2[:, :], 1.0, None, ALU.add))
            c.sync()
            c.put(v.reciprocal(s3[:, :], s3[:, :]))
            c.sync()
            c.put(v.tensor_scalar(dg[:, :], k.ident[:, :], s3[:, :], None, ALU.mult))
            v.wait_ge(squeeze_pe, 3)
            c.put(v.tensor_copy(k.srow[:, :], pr[:, 0:P]))
            c.sync()

            def gated(st):
                s = st.slot
                v.wait_ge(rows_in[s], 32 * (st.k + 1))
                need(v, rows_out[s], 16 * st.k)
                v.tensor_tensor(O[:, s], Y[:, s], k.srow[:, :].unsqueeze(1).to_broadcast([P, J, P]), ALU.mult).then_inc(mults, 1)
                v.wait_ge(mults, st.m + 1)
                v.tensor_tensor(O[:, s], O[:, s], X[:, s], ALU.add).then_inc(sums, 1)

            run_steps(v, NG, [(0, gated)])

        blocks.close()
        clear_semaphores(nc, used)


class Shared:
    pass


def build(nc, N, E, a):
    T = E // EP
    assert T * EP == E and T % B == 0
    NG = -(-N // GROUP)
    TAIL = N - (NG - 1) * GROUP
    NB = T // B
    assert TAIL % J == 0 and N >= GROUP

    def table(name, rows=N):
        return nc.dram_tensor(name, (rows, P), F32).ap()

    h1_t, x1_t, y2_t = (table(n) for n in ("tab_h1", "tab_x1", "tab_y2"))
    xx_t = nc.dram_tensor("tab_xx", (N, 2 * P), F32).ap()
    xe_t = nc.dram_tensor("tab_xe", (E, P), F32).ap()
    dr1_t, dr2_t = table("tab_dr1", E), table("tab_dr2", E)
    ZR = -(-NG * GROUP // (NB * P)) * P
    z_rows = NB * ZR
    z_t = table("tab_z", z_rows)

    def rows_of(t, st):
        base = N - GROUP if st.last else st.m * GROUP
        return t[bass.ds(base, GROUP), :].rearrange("(p j) f -> p j f", j=J)

    whole = ExitStack()
    with whole:
        def sb(name, shape, dt=F32, ctx=whole):
            return ctx.enter_context(nc.sbuf_tensor(name, list(shape), dt))

        def pb(name, ctx):
            return ctx.enter_context(nc.psum_tensor(name, [P, 512], F32))

        used = []

        def sem(name, ctx):
            used.append(ctx.enter_context(nc.semaphore(name)))
            return used[-1]

        ident = sb("ident", [P, P])
        ones = sb("ones", [P, P])
        tail_ones = sb("tail_ones", [P, 1])
        half = sb("half", [P, 2 * B])
        headmask = sb("headmask", [P, 4])
        W = {n: sb(n, [P, P]) for n in ("W1l", "W1r", "W2l", "W2r", "WQT", "WKT", "WVT", "WET")}
        WS6 = sb("WS6", [6, P])
        WG6 = sb("WG6", [6, P])
        att = [sb("att1c", [P, 4]), sb("att2c", [P, 4])]
        col = {n: sb("c_" + n, [P, 1]) for n in ("b1", "b2", "ln1_g", "ln1_b", "ln2_g", "ln2_b", "w_a", "ffn_b2", "se_b2", "a1", "a2")}
        fb1 = sb("fb1", [P, 4])
        seb1 = sb("seb1", [32, 1])
        F1T = sb("F1T", [P, 4, P])
        F2T = sb("F2T", [P, 4, P])
        S1T = sb("S1T", [P, 32])
        S2T = sb("S2T", [32, P])
        row = {n: sb("r_" + n, [P, P]) for n in ("b1", "b2", "w_g", "b_g")}
        idx = sb("idx", [EP, T, 6], I32)
        flag = sb("flag", [EP, T, 10])
        idxP = sb("idxP", [EP, 2], I32)
        idxQ = sb("idxQ", [EP, 2], I32)
        idxE = sb("idxE", [EP, 2], I32)
        ET = sb("ET", [EP, EP])
        EA = sb("EA", [EP, EP])
        EB = sb("EB", [EP, EP])
        EF = sb("EF", [EP, EP])
        NF, NA = sb("NF", [EP, EP]), sb("NA", [EP, EP])
        NT = sb("NT", [EP, EP])
        NBm = sb("NBm", [EP, EP])
        srow = sb("srow", [P, P])
        gsum = sb("gsum", [P, 1])

        with ExitStack() as ctx, ExitStack() as blocks:
            raw = {n: sb("raw_" + n, [P, P], ctx=ctx) for n in ("WQ", "WK", "WV", "WE")}
            rawS = sb("rawS", [P, 6], ctx=ctx)
            raw1 = sb("raw1", [P, 4, P], ctx=ctx)
            raw2 = sb("raw2", [P, 512], ctx=ctx)
            rawe1 = sb("rawe1", [32, P], ctx=ctx)
            rawe2 = sb("rawe2", [P, 32], ctx=ctx)
            dint = sb("dint", [EP, T + 2], I32, ctx)
            sint = sb("sint", [EP, T], I32, ctx)
            d = sb("d", [EP, T + 2], ctx=ctx)
            stt, ent, hrt, het, wrt, tmp = (sb(n, [EP, T], ctx=ctx) for n in ("stt", "ent", "hrt", "het", "wrt", "tmp"))
            trt, tet, wrb = (sb(n, [EP, T], ctx=ctx) for n in ("trt", "tet", "wrb"))
            sm = sb("sm", [EP, 16], ctx=ctx)
            tri = sb("tri", [EP, EP], ctx=ctx)
            dg = sb("dg", [EP, 2, EP], ctx=ctx)
            drow = sb("drow", [EP, 2, EP], ctx=ctx)
            ps = [pb(f"ps{i}", ctx) for i in range(6)]
            loaded = sem("setup_loaded", ctx)
            edges_in = sem("edges_in", ctx)
            pads = sem("pads", ctx)
            made = sem("consts_made", ctx)
            madeg = sem("consts_steps", ctx)
            turned = sem("weights_turned", ctx)
            vec = sem("setup_vec", ctx)
            diag = sem("diag_ready", ctx)
            drows = sem("drows_ready", ctx)
            copied = sem("weights_copied", ctx)
            block = blocks.enter_context(nc.Block())
            loads = []

            def column(v):
                return v.rearrange("(f a) -> f a", a=1)

            loads += [(W["W1l"][:, :], a["L0_gnn_W1_l"]), (W["W1r"][:, :], a["L0_gnn_W1_r"]),
                      (W["W2l"][:, :], a["L0_gnn_W2_l"]), (W["W2r"][:, :], a["L0_gnn_W2_r"])]
            loads += [(raw[n][:, :], a["L1_gnn_" + n]) for n in raw]
            loads += [(rawS[:, 2:6], a["L1_gnn_WS"]), (rawe1[:, :], a["L1_gnn_se_w1"]), (rawe2[:, :], a["L1_gnn_se_w2"]),
                      (raw1[:, :, :], a["L1_gnn_ffn_w1"].rearrange("(c p) n -> p c n", p=P)), (raw2[:, :], a["L1_gnn_ffn_w2"])]
            loads += [(col["b1"][:, :], column(a["L0_gnn_b1"])), (col["b2"][:, :], column(a["L0_gnn_b2"])),
                      (col["a1"][:, :], a["L0_gnn_att1"].rearrange("h (c a) -> (h c) a", a=1)),
                      (col["a2"][:, :], a["L0_gnn_att2"].rearrange("h (c a) -> (h c) a", a=1)),
                      (seb1[:, :], column(a["L1_gnn_se_b1"])),
                      (fb1[:, :], a["L1_gnn_ffn_b1"].rearrange("(c p) -> p c", p=P))]
            loads += [(col[n][:, :], column(a["L1_gnn_" + n])) for n in ("ln1_g", "ln1_b", "ln2_g", "ln2_b", "w_a", "ffn_b2", "se_b2")]
            loads += [(row["b1"][:, :], a["L0_gnn_b1"].partition_broadcast(P)), (row["b2"][:, :], a["L0_gnn_b2"].partition_broadcast(P)),
                      (row["w_g"][:, :], a["L1_gnn_w_g"].partition_broadcast(P)), (row["b_g"][:, :], a["L1_gnn_b_g"].partition_broadcast(P))]
            loads += [(WG6[0:1, :], a["L1_gnn_w_g"].partition_broadcast(1)), (WG6[1:2, :], a["L1_gnn_b_g"].partition_broadcast(1))]

            @block.sync
            def _(sp):
                dst2 = a["dst"].rearrange("(p t) -> p t", t=T)
                sp.wait_ge(pads, 3)
                sp.dma_start(dint[:, 1:T + 1], dst2).then_inc(edges_in, 16)
                sp.dma_start(dint[1:EP, 0:1], dst2[0:EP - 1, T - 1:T], allow_slow_non_contiguous=True).then_inc(edges_in, 16)
                sp.dma_start(dint[0:EP - 1, T + 1:T + 2], dst2[1:EP, 0:1], allow_slow_non_contiguous=True).then_inc(edges_in, 16)
                sp.dma_start(sint[:, :], a["src"].rearrange("(p t) -> p t", t=T)).then_inc(edges_in, 16)
                sp.wait_ge(pads, 3)
                for to, of in loads:
                    sp.dma_start(to, of, allow_slow_non_contiguous=True).then_inc(loaded, 16)

            @block.gpsimd
            def _(pool):
                pool.memset(dint[:, :], -1).then_inc(pads, 1)
                pool.memset(WG6[:, :], 0.0).then_inc(pads, 1)
                pool.memset(rawS[:, :], 0.0).then_inc(pads, 1)
                c = Chain(pool, madeg)
                c.put(pool.memset(ident[:, :], 0.0))
                c.put(pool.memset(ones[:, :], 1.0))
                c.put(pool.memset(tail_ones[:, :], 1.0))
                c.put(pool.memset(headmask[:, :], 1.0))
                c.put(pool.memset(half[:, :], -0.5))
                c.put(pool.memset(tri[:, :], 1.0))
                c.sync()
                c.put(pool.affine_select(out=ident[:, :], in_=ident[:, :], compare_op=ALU.not_equal, fill=1.0,
                                         base=0, pattern=[[-1, P]], channel_multiplier=1))
                c.put(pool.affine_select(out=tail_ones[:, :], in_=tail_ones[:, :], compare_op=ALU.is_ge, fill=0.0,
                                         base=-(GROUP - TAIL), pattern=[[0, 1]], channel_multiplier=J))
                c.put(pool.affine_select(out=tri[:, :], in_=tri[:, :], compare_op=ALU.is_ge, fill=0.0,
                                         base=-1, pattern=[[-1, EP]], channel_multiplier=1))
                c.put(pool.affine_select(out=headmask[:, :], in_=headmask[:, :], compare_op=ALU.is_ge, fill=0.0,
                                         base=0, pattern=[[-32, 4]], channel_multiplier=1))
                c.sync()
                c.put(pool.affine_select(out=headmask[:, :], in_=headmask[:, :], compare_op=ALU.is_ge, fill=0.0,
                                         base=31, pattern=[[32, 4]], channel_multiplier=-1))
                c.sync()
                pool.sem_inc(made, 1)

            @block.tensor
            def _(pe):
                pe.wait_ge(made, 1)
                pe.wait_ge(loaded, 16 * len(loads))
                idt = ident[:, :]
                for i, n in enumerate(("WQ", "WK", "WV", "WE")):
                    nc.tensor.transpose(ps[0][:, i * P:(i + 1) * P], raw[n][:, :], idt)
                for i in range(4):
                    nc.tensor.transpose(ps[1][:, i * P:(i + 1) * P], raw1[:, i, :], idt)
                    nc.tensor.transpose(ps[2][:, i * P:(i + 1) * P], raw2[:, i * P:(i + 1) * P], idt)
                nc.tensor.transpose(ps[3][0:6, 0:P], rawS[:, :], idt)
                nc.tensor.transpose(ps[3][:, P:P + 32], rawe1[:, :], ident[0:32, 0:32])
                nc.tensor.transpose(ps[3][0:32, 2 * P:3 * P], rawe2[:, :], idt).then_inc(turned, 1)
                pe.wait_ge(diag, 1)
                for i in range(2):
                    last = nc.tensor.matmul(ps[4][0:EP, i * EP:(i + 1) * EP], ones[0:EP, 0:EP], dg[:, i, :], start=True, stop=True)
                last.then_inc(drows, 1)

            @block.scalar
            def _(act):
                act.wait_ge(turned, 1)
                for i, n in enumerate(("WQT", "WKT", "WVT", "WET")):
                    act.activation(W[n][:, :], ps[0][:, i * P:(i + 1) * P], ACT.Copy)
                act.activation(F1T[:, :, :], ps[1][:, :].rearrange("p (c n) -> p c n", c=4), ACT.Copy)
                act.activation(F2T[:, :, :], ps[2][:, :].rearrange("p (c n) -> p c n", c=4), ACT.Copy)
                act.activation(WS6[:, :], ps[3][0:6, 0:P], ACT.Copy)
                act.activation(S1T[:, :], ps[3][:, P:P + 32], ACT.Copy)
                act.activation(S2T[:, :], ps[3][0:32, 2 * P:3 * P], ACT.Copy).then_inc(copied, 1)
                act.wait_ge(copied, 1)

            @block.vector
            def _(v):
                c = Chain(v, vec)
                v.wait_ge(made, 1)
                v.wait_ge(loaded, 16 * len(loads))
                for i, n in enumerate(("a1", "a2")):
                    c.put(v.tensor_scalar(att[i][:, :], headmask[:, :], col[n][:, :], None, ALU.mult))
                v.wait_ge(edges_in, 64)
                c.put(v.tensor_copy(d[:, :], dint[:, :]))
                c.put(v.tensor_copy(idx[:, :, 0], sint[:, :]))
                c.put(v.tensor_copy(idx[:, :, 1], dint[:, 1:T + 1]))
                c.put(v.tensor_scalar(idx[:, :, 2], sint[:, :], 2.0, None, ALU.mult))
                c.put(v.tensor_copy(idx[:, :, 3], dint[:, 1:T + 1]))
                c.sync()
                now = d[:, 1:T + 1]
                c.put(v.tensor_tensor(stt[:, :], now, d[:, 0:T], ALU.not_equal))
                c.put(v.tensor_tensor(ent[:, :], now, d[:, 2:T + 2], ALU.not_equal))
                c.put(v.tensor_scalar(dg[:, 0, :], ident[0:EP, 0:EP], d[:, T:T + 1], None, ALU.mult))
                c.put(v.tensor_scalar(dg[:, 1, :], ident[0:EP, 0:EP], d[:, 1:2], None, ALU.mult))
                c.sync()
                c.put(v.tensor_scalar(sm[:, 0:1], stt[:, 0:1], -1.0, 1.0, ALU.mult, ALU.add))
                c.put(v.tensor_scalar(sm[:, 4:5], ent[:, T - 1:T], -1.0, 1.0, ALU.mult, ALU.add))
                v.sem_inc(diag, 1)
                c.sync()
                c.put(v.tensor_scalar(hrt[:, :], now, d[:, 1:2], sm[:, 0:1], ALU.is_equal, ALU.mult))
                c.put(v.tensor_scalar(trt[:, :], now, d[:, T:T + 1], sm[:, 4:5], ALU.is_equal, ALU.mult))
                c.put(v.tensor_copy(flag[:, :, 0], stt[:, :]))
                c.put(v.tensor_scalar(flag[:, :, 1], stt[:, :], -1.0, 1.0, ALU.mult, ALU.add))
                c.put(v.tensor_scalar(flag[:, :, 2], stt[:, :], NEG, None, ALU.mult))
                c.put(v.tensor_scalar(flag[:, :, 3], stt[:, :], 1.0, -NEG, ALU.subtract, ALU.mult))
                c.put(v.tensor_scalar(flag[:, :, 5], ent[:, :], NEG, None, ALU.mult))
                c.put(v.tensor_scalar(flag[:, :, 6], stt[:, :], 1.0, -NEG, ALU.subtract, ALU.mult))
                c.put(v.tensor_copy(flag[:, :, 8], ent[:, :]))
                c.put(v.tensor_scalar(flag[:, :, 9], ent[:, :], -1.0, 1.0, ALU.mult, ALU.add))
                c.sync()
                c.put(v.memset(flag[:, 0, 0:1], 1.0))
                c.put(v.memset(flag[:, 0, 1:2], 0.0))
                c.put(v.memset(flag[:, 0, 2:3], NEG))
                c.put(v.memset(flag[:, T - 1, 5:6], NEG))
                c.put(v.memset(flag[:, T - 1, 8:9], 1.0))
                c.put(v.memset(flag[:, T - 1, 9:10], 0.0))
                c.put(v.tensor_tensor(het[:, :], hrt[:, :], ent[:, :], ALU.mult))
                c.put(v.tensor_tensor(tet[:, :], trt[:, :], stt[:, :], ALU.mult))
                c.put(v.tensor_reduce(sm[:, 5:6], hrt[:, :], AX.X, ALU.add))
                c.put(v.tensor_reduce(sm[:, 6:7], trt[:, :], AX.X, ALU.add))
                c.put(v.tensor_reduce(sm[:, 7:8], tri[:, :], AX.X, ALU.add))
                c.sync()
                c.put(v.tensor_tensor(wrt[:, :], ent[:, :], het[:, :], ALU.subtract))
                c.put(v.tensor_tensor(wrb[:, :], stt[:, :], tet[:, :], ALU.subtract))
                c.put(v.scalar_tensor_tensor(sm[:, 8:9], sm[:, 7:8], float(T), sm[:, 5:6], ALU.mult, ALU.add))
                c.put(v.scalar_tensor_tensor(sm[:, 9:10], sm[:, 7:8], float(T), sm[:, 6:7], ALU.mult, ALU.subtract))
                c.sync()
                c.put(v.memset(het[:, T - 1:T], 0.0))
                c.put(v.memset(wrt[:, T - 1:T], 0.0))
                c.put(v.memset(tet[:, 0:1], 0.0))
                c.put(v.memset(wrb[:, 0:1], 0.0))
                c.sync()
                c.put(v.tensor_copy(flag[:, :, 4], het[:, :]))
                c.put(v.tensor_copy(flag[:, :, 7], tet[:, :]))
                c.put(v.tensor_scalar(tmp[:, :], wrt[:, :], -SKIP, SKIP, ALU.mult, ALU.add))
                c.put(v.tensor_scalar(hrt[:, :], wrb[:, :], -SKIP, SKIP, ALU.mult, ALU.add))
                c.put(v.tensor_reduce(sm[:, 1:2], het[:, :], AX.X, ALU.max))
                c.put(v.tensor_reduce(sm[:, 10:11], tet[:, :], AX.X, ALU.max))
                c.sync()
                c.put(v.tensor_tensor(idx[:, :, 4], tmp[:, :], now, ALU.add))
                c.put(v.tensor_tensor(idx[:, :, 5], hrt[:, :], now, ALU.add))
                c.put(v.tensor_scalar(sm[:, 2:3], sm[:, 1:2], -SKIP, SKIP, ALU.mult, ALU.add))
                c.put(v.tensor_scalar(sm[:, 3:4], ent[:, T - 1:T], -SKIP, SKIP, ALU.mult, ALU.add))
                c.put(v.tensor_scalar(sm[:, 11:12], sm[:, 10:11], -SKIP, SKIP, ALU.mult, ALU.add))
                c.put(v.tensor_scalar(sm[:, 12:13], stt[:, 0:1], -SKIP, SKIP, ALU.mult, ALU.add))
                c.sync()
                c.put(v.tensor_tensor(idxP[:, 0:1], sm[:, 3:4], d[:, T:T + 1], ALU.add))
                c.put(v.tensor_tensor(idxP[:, 1:2], sm[:, 2:3], d[:, 1:2], ALU.add))
                c.put(v.tensor_tensor(idxQ[:, 0:1], sm[:, 12:13], d[:, 1:2], ALU.add))
                c.put(v.tensor_tensor(idxQ[:, 1:2], sm[:, 11:12], d[:, T:T + 1], ALU.add))
                c.put(v.scalar_tensor_tensor(idxE[:, 0:1], sm[:, 8:9], -1.0, sm[:, 2:3], ALU.add, ALU.add))
                c.put(v.scalar_tensor_tensor(idxE[:, 1:2], sm[:, 9:10], float(T), sm[:, 11:12], ALU.add, ALU.add))
                v.wait_ge(drows, 1)
                c.put(v.tensor_copy(drow[:, :, :], ps[4][0:EP, 0:2 * EP].rearrange("p (a q) -> p a q", a=2)))
                c.sync()
                c.put(v.tensor_scalar(ET[:, :], drow[:, 0, :], d[:, T:T + 1], None, ALU.is_equal))
                c.put(v.tensor_scalar(EA[:, :], drow[:, 1, :], d[:, T:T + 1], None, ALU.is_equal))
                c.put(v.tensor_scalar(EB[:, :], drow[:, 0, :], d[:, 1:2], None, ALU.is_equal))
                c.put(v.tensor_scalar(EF[:, :], drow[:, 1, :], d[:, 1:2], None, ALU.is_equal))
                c.sync()
                c.put(v.tensor_scalar(NT[:, :], ET[:, :], 1.0, -NEG, ALU.subtract, ALU.mult))
                c.put(v.tensor_scalar(NF[:, :], EF[:, :], 1.0, -NEG, ALU.subtract, ALU.mult))
                c.put(v.tensor_scalar(NA[:, :], EA[:, :], 1.0, -NEG, ALU.subtract, ALU.mult))
                c.put(v.tensor_scalar(NBm[:, :], EB[:, :], 1.0, -NEG, ALU.subtract, ALU.mult))
                c.sync()

            blocks.close()
            clear_semaphores(nc, used)
            used.clear()

        with ExitStack() as ctx, ExitStack() as blocks:
            X = sb("X", [P, 2 * SLOTS, J, 2 * P], ctx=ctx)
            H1N = sb("H1N", [P, SLOTS, J, P], ctx=ctx)
            X1 = sb("X1", [P, SLOTS, J, P], ctx=ctx)
            bn = sb("bn", [P, SLOTS, J, 6], ctx=ctx)
            mean = sb("mean", [P, SLOTS, J], ctx=ctx)
            vpe = sb("vpe", [P, SLOTS, J], ctx=ctx)
            tmpm = sb("tmpm", [P, 3, J], ctx=ctx)
            rstd = sb("rstd", [P, SLOTS, J], ctx=ctx)
            h0T, h1T, h2T = (sb(n, [P, 2, GROUP], ctx=ctx) for n in ("h0T", "h1T", "h2T"))
            pT0, pM1, pM2, pN1, pN2 = (pb(n, ctx) for n in ("pT0", "pM1", "pM2", "pN1", "pN2"))
            x_in = [sem(f"x_in{s}", ctx) for s in range(2 * SLOTS)]
            xx_out = [sem(f"xx_out{s}", ctx) for s in range(2 * SLOTS)]
            h1_out = [sem(f"h1_out{s}", ctx) for s in range(SLOTS)]
            x1_out = [sem(f"x1_out{s}", ctx) for s in range(SLOTS)]
            K_TAKE = J + 7
            names = ("moments_steps", "rstd_ready", "xn_ready", "x1_ready", "tr0", "mm1", "mm2", "tr1", "tr2",
                     "h0T_ready", "h1T_ready", "h1N_ready", "h2T_ready")
            (moments_steps, rstd_ready, xn_ready, x1_ready, tr0, mm1, mm2, tr1, tr2,
             h0T_ready, h1T_ready, h1N_ready, h2T_ready) = (sem(n, ctx) for n in names)
            block = blocks.enter_context(nc.Block())

            @block.sync
            def _(sp):
                def load(st):
                    need(sp, x1_ready, st.m - 7)
                    need(sp, xx_out[st.wslot], 16 * st.wk)
                    sp.dma_start(X[:, st.wslot, :, P:2 * P], rows_of(a["x"], st)).then_inc(x_in[st.wslot], 16)

                def store_xx(st):
                    sp.wait_ge(xn_ready, st.m + 1)
                    if st.last:
                        sp.wait_ge(xx_out[(st.m - 1) % (2 * SLOTS)], 16 * ((st.m - 1) // (2 * SLOTS) + 1))
                    sp.dma_start(rows_of(xx_t, st), X[:, st.wslot]).then_inc(xx_out[st.wslot], 16)

                def store(ready, buf, tab, done):
                    def fn(st):
                        sp.wait_ge(ready, st.m + 1)
                        if st.last:
                            sp.wait_ge(done[(st.m - 1) % SLOTS], 16 * ((st.m - 1) // SLOTS + 1))
                        sp.dma_start(rows_of(tab, st), buf[:, st.slot]).then_inc(done[st.slot], 16)
                    return fn

                run_steps(sp, NG, [(0, load), (3, store_xx), (6, store(h1N_ready, H1N, h1_t, h1_out)),
                                   (8, store(x1_ready, X1, x1_t, x1_out))], 2 * SLOTS)
                for done in (xx_out, h1_out, x1_out):
                    for s in range(len(done)):
                        sp.wait_ge(done[s], 16 * ((NG - 1 - s) // len(done) + 1))

            @block.gpsimd
            def _(pool):
                def rsqrt(st):
                    pool.wait_ge(moments_steps, (st.m + 1) * K_TAKE)
                    pool.tensor_tensor(rstd[:, st.slot], vpe[:, st.slot], half[:, 0:J], ALU.pow).then_inc(rstd_ready, 1)

                run_steps(pool, NG, [(0, rsqrt)])

            @block.vector
            def _(v):
                cm = Chain(v, moments_steps)

                def take_stats(st):
                    v.wait_ge(x_in[st.wslot], 16 * (st.wk + 1))
                    need(v, moments_steps, st.m * K_TAKE)
                    c = cm.at(st.m * K_TAKE)
                    for j in range(J):
                        c.put(v.bn_stats(bn[:, st.slot, j], X[:, st.wslot, j, P:2 * P]))
                    c.sync()
                    moments(v, c, bn[:, st.slot], mean[:, st.slot], vpe[:, st.slot], tmpm)
                    assert c.n == K_TAKE

                def normalise(st):
                    v.wait_ge(rstd_ready, st.m + 1)
                    need(v, tr0, st.m - 7)
                    for j in range(J):
                        last = v.tensor_scalar(X[:, st.wslot, j, 0:P], X[:, st.wslot, j, P:2 * P], mean[:, st.slot, j:j + 1],
                                               rstd[:, st.slot, j:j + 1], ALU.subtract, ALU.mult)
                    last.then_inc(xn_ready, 1)

                def residual(st):
                    v.wait_ge(tr2, st.m + 1)
                    need(v, x1_out[st.slot], 16 * st.k)
                    v.tensor_tensor(X1[:, st.slot], X[:, st.wslot, :, P:2 * P], pN2[:, :].rearrange("p (j f) -> p j f", j=J),
                                    ALU.add).then_inc(x1_ready, 1)

                run_steps(v, NG, [(2, normalise), (6, residual), (0, take_stats)], 2 * SLOTS)

            @block.tensor
            def _(pe):
                def turn_x(st):
                    pe.wait_ge(xn_ready, st.m + 1)
                    need(pe, h0T_ready, st.m)
                    for j in range(J):
                        last = nc.tensor.transpose(pT0[:, j * P:(j + 1) * P], X[:, st.wslot, j, 0:P], ident[:, :])
                    last.then_inc(tr0, 1)

                def layer1(st):
                    pe.wait_ge(h0T_ready, st.m + 1)
                    need(pe, h1T_ready, st.m)
                    nc.tensor.matmul(pM1[:, :], W["W1l"][:, :], h0T[:, st.slot % 2], start=True, stop=True).then_inc(mm1, 1)

                def layer2(st):
                    pe.wait_ge(h1T_ready, st.m + 1)
                    need(pe, h2T_ready, st.m)
                    nc.tensor.matmul(pM2[:, :], W["W2l"][:, :], h1T[:, st.slot % 2], start=True, stop=True).then_inc(mm2, 1)
                    need(pe, h1N_ready, st.m)
                    for j in range(J):
                        last = nc.tensor.transpose(pN1[:, j * P:(j + 1) * P], h1T[:, st.slot % 2, j * P:(j + 1) * P], ident[:, :])
                    last.then_inc(tr1, 1)

                def turn_h2(st):
                    pe.wait_ge(h2T_ready, st.m + 1)
                    need(pe, x1_ready, st.m)
                    for j in range(J):
                        last = nc.tensor.transpose(pN2[:, j * P:(j + 1) * P], h2T[:, st.slot % 2, j * P:(j + 1) * P], ident[:, :])
                    last.then_inc(tr2, 1)

                run_steps(pe, NG, [(0, turn_x), (3, turn_h2), (1, layer1), (2, layer2)], 2 * SLOTS)

            @block.scalar
            def _(act):
                def relu_x(st):
                    act.wait_ge(tr0, st.m + 1)
                    need(act, mm1, st.m - 1)
                    act.activation(h0T[:, st.slot % 2], pT0[:, :], ACT.Relu).then_inc(h0T_ready, 1)

                def relu_h1(st):
                    act.wait_ge(mm1, st.m + 1)
                    need(act, tr1, st.m - 1)
                    act.activation(h1T[:, st.slot % 2], pM1[:, :], ACT.Relu, bias=col["b1"][:, :]).then_inc(h1T_ready, 1)

                def copy_h1(st):
                    act.wait_ge(tr1, st.m + 1)
                    need(act, h1_out[st.slot], 16 * st.k)
                    act.activation(H1N[:, st.slot], pN1[:, :].rearrange("p (j f) -> p j f", j=J), ACT.Copy).then_inc(h1N_ready, 1)

                def relu_h2(st):
                    act.wait_ge(mm2, st.m + 1)
                    need(act, tr2, st.m - 1)
                    act.activation(h2T[:, st.slot % 2], pM2[:, :], ACT.Relu, bias=col["b2"][:, :]).then_inc(h2T_ready, 1)

                run_steps(act, NG, [(0, relu_x), (1, relu_h1), (2, relu_h2), (2, copy_h1)])

            blocks.close()
            clear_semaphores(nc, used)

        k = Shared()
        k.EA, k.ET, k.F1T, k.F2T, k.N, k.NB, k.NBm, k.NG, k.NT, k.S1T = EA, ET, F1T, F2T, N, NB, NBm, NG, NT, S1T
        k.S2T, k.T, k.W, k.WS6, k.ZR, k.a, k.col, k.fb1, k.flag, k.gsum = S2T, T, W, WS6, ZR, a, col, fb1, flag, gsum
        k.half, k.ident, k.idx, k.idxP, k.ones, k.row, k.rows_of, k.seb1, k.srow, k.tail_ones = half, ident, idx, idxP, ones, row, rows_of, seb1, srow, tail_ones
        k.WG6 = WG6
        k.whole, k.by_pool_dma = whole, ("gat", "rows_out", "join_in", "join_out", "ends_in", "ends_scattered")
        k.E, k.EB, k.EF, k.NF, k.NA, k.idxQ, k.idxE = E, EB, EF, NF, NA, idxQ, idxE
        k.dst_rows = [dr1_t, dr2_t]
        k.x1_t, k.y2_t, k.z_rows, k.z_t, k.xe_t = x1_t, y2_t, z_rows, z_t, xe_t
        gat_layer(nc, k, 1, xx_t.rearrange("n (a f) -> (n a) f", a=2), xx_t, h1_t, None, W["W1l"], W["W1r"], att[0], row["b1"])
        gat_layer(nc, k, 2, h1_t, h1_t, x1_t, a["x"], W["W2l"], W["W2r"], att[1], row["b2"])
        edge_attention(nc, k)
        ffn_pass(nc, k)
        squeeze_and_out(nc, k)


_INS = ["x", "src", "dst", "L0_gnn_W1_l", "L0_gnn_W1_r", "L0_gnn_att1", "L0_gnn_b1", "L0_gnn_W2_l", "L0_gnn_W2_r", "L0_gnn_att2",
        "L0_gnn_b2", "L1_gnn_ln1_g", "L1_gnn_ln1_b", "L1_gnn_ln2_g", "L1_gnn_ln2_b", "L1_gnn_WQ", "L1_gnn_WK", "L1_gnn_WV",
        "L1_gnn_WS", "L1_gnn_WE", "L1_gnn_w_a", "L1_gnn_w_g", "L1_gnn_b_g", "L1_gnn_ffn_w1", "L1_gnn_ffn_b1", "L1_gnn_ffn_w2",
        "L1_gnn_ffn_b2", "L1_gnn_se_w1", "L1_gnn_se_b1", "L1_gnn_se_w2", "L1_gnn_se_b2"]


def kernel(**inputs):
    import numpy as _np
    import concourse.bacc as _bacc
    from concourse import mybir as _mybir
    from concourse.bass_utils import run_bass_kernel_spmd as _run

    nc = _bacc.Bacc("TRN2", target_bir_lowering=False, num_devices=1)
    arrays, args = {}, {}
    for name in _INS:
        v = _np.ascontiguousarray(inputs[name])
        arrays[f"in_{name}"] = v
        args[name] = nc.dram_tensor(f"in_{name}", v.shape, _mybir.dt.from_np(v.dtype), kind="ExternalInput").ap()
    n, e = inputs["x"].shape[0], inputs["src"].shape[0]
    args["out"] = nc.dram_tensor("out_0", (n, P), _mybir.dt.float32, kind="ExternalOutput").ap()
    build(nc, n, e, args)
    r = _run(nc, [arrays], core_ids=[0])
    return r.results[0]["out_0"]
```
